# Optimizing a Trainium2 kernel written in Bass

```python
import numpy as np
import jax
import jax.numpy as jnp

def _softmax(x, axis=-1):
    return jax.nn.softmax(x, axis=axis)

def _gelu(x):
    return jax.nn.gelu(x, approximate=True)

def _silu(x):
    return jax.nn.silu(x)

def _sigmoid(x):
    return jax.nn.sigmoid(x)

def _layernorm(x, axis=-1, eps=1e-05):
    m = jnp.mean(x, axis=axis, keepdims=True)
    v = jnp.var(x, axis=axis, keepdims=True)
    return (x - m) / jnp.sqrt(v + eps)

def _scatter_add(tgt, idx, src, axis=0):
    return tgt.at[idx].add(src)

def _segment_sum(src, seg, n):
    return jax.ops.segment_sum(src, seg, n)
kernel_name = 'mk_seq_postln_d1_jaxref_r8_3d908b'

def setup_inputs(seed: int=0):
    np.random.seed(seed)
    _w = jnp.asarray

    def _L0_attn_setup():
        import jax, jax.numpy as jnp
        import numpy as np
        B, L, D_MODEL = (4, 256, 128)
        D_INNER = 2 * D_MODEL
        D_STATE = 64
        D_CONV = 4
        DT_RANK = D_MODEL // 16

        def _mamba_block(x, ln_w, ln_b, W_in, conv_w, conv_b, W_xproj, W_dt, b_dt, A_log, D, W_out):
            residual = x
            mu = jnp.mean(x, axis=-1, keepdims=True)
            var = jnp.mean(jnp.square(x - mu), axis=-1, keepdims=True)
            xn = (x - mu) * jax.lax.rsqrt(var + 1e-05) * ln_w + ln_b
            xz = xn @ W_in
            xi, z = jnp.split(xz, 2, axis=-1)
            xc = jnp.transpose(xi, (0, 2, 1))
            xc = jax.lax.conv_general_dilated(xc, conv_w, window_strides=(1,), padding=[(D_CONV - 1, 0)], feature_group_count=D_INNER, dimension_numbers=('NCH', 'OIH', 'NCH'))
            xc = jnp.transpose(xc, (0, 2, 1)) + conv_b
            u = jax.nn.silu(xc)
            x_dbl = u @ W_xproj
            dt_r = x_dbl[..., :DT_RANK]
            Bm = x_dbl[..., DT_RANK:DT_RANK + D_STATE]
            Cm = x_dbl[..., DT_RANK + D_STATE:]
            delta = jax.nn.softplus(dt_r @ W_dt + b_dt)
            A = -jnp.exp(A_log)

            def step(h, inputs):
                d_t, B_t, C_t, u_t = inputs
                dA = jnp.exp(d_t[:, :, None] * A)
                h = h * dA + (d_t * u_t)[:, :, None] * B_t[:, None, :]
                y_t = jnp.einsum('bdn,bn->bd', h, C_t)
                return (h, y_t)
            h0 = jnp.zeros((x.shape[0], D_INNER, D_STATE), x.dtype)
            seq = (jnp.transpose(delta, (1, 0, 2)), jnp.transpose(Bm, (1, 0, 2)), jnp.transpose(Cm, (1, 0, 2)), jnp.transpose(u, (1, 0, 2)))
            _, ys = jax.lax.scan(step, h0, seq)
            y = jnp.transpose(ys, (1, 0, 2)) + u * D
            y = y * jax.nn.silu(z)
            out = y @ W_out
            return residual + out
        key = jax.random.key(seed)
        ks = jax.random.split(key, 10)
        inp = {}
        inp['x'] = jax.random.normal(ks[0], (B, L, D_MODEL), dtype=jnp.float32)
        inp['ln_w'] = jnp.ones((D_MODEL,), jnp.float32)
        inp['ln_b'] = jnp.zeros((D_MODEL,), jnp.float32)
        inp['W_in'] = jax.random.normal(ks[1], (D_MODEL, 2 * D_INNER), jnp.float32) / np.sqrt(D_MODEL)
        inp['conv_w'] = jax.random.normal(ks[2], (D_INNER, 1, D_CONV), jnp.float32) / np.sqrt(D_CONV)
        inp['conv_b'] = jax.random.normal(ks[3], (D_INNER,), jnp.float32) * 0.01
        inp['W_xproj'] = jax.random.normal(ks[4], (D_INNER, DT_RANK + 2 * D_STATE), jnp.float32) / np.sqrt(D_INNER)
        inp['W_dt'] = jax.random.normal(ks[5], (DT_RANK, D_INNER), jnp.float32) / np.sqrt(DT_RANK)
        inp['b_dt'] = jax.random.normal(ks[6], (D_INNER,), jnp.float32) * 0.1 - 4.0
        inp['A_log'] = jnp.log(jnp.broadcast_to(jnp.arange(1, D_STATE + 1, dtype=jnp.float32), (D_INNER, D_STATE)))
        inp['D'] = jnp.ones((D_INNER,), jnp.float32)
        inp['W_out'] = jax.random.normal(ks[7], (D_INNER, D_MODEL), jnp.float32) / np.sqrt(D_INNER)
        return inp
    _L0_attn_in = _L0_attn_setup()

    def _L0_ffn_setup():
        import jax, jax.numpy as jnp
        import numpy as np
        L, E, H, F, K = (4, 4, 128, 512, 2)
        B, S = (4, 256)
        EPS = 1e-05

        def _moe_layer(x, rw, rb, g, b, w1, b1, w2, b2):
            logits = jnp.einsum('bsh,he->bse', x, rw) + rb
            probs = jax.nn.softmax(logits, axis=-1)
            vals, idx = jax.lax.top_k(probs, K)
            vals = vals / vals.sum(axis=-1, keepdims=True)
            mu = x.mean(axis=-1, keepdims=True)
            xc = x - mu
            xhat = xc * jax.lax.rsqrt((xc * xc).mean(axis=-1, keepdims=True) + EPS)
            xe = xhat[None] * g[:, None, None, :] + b[:, None, None, :]
            h = jax.nn.gelu(jnp.einsum('ebsh,ehf->ebsf', xe, w1) + b1[:, None, None, :], approximate=False)
            y = jnp.einsum('ebsf,efh->ebsh', h, w2) + b2[:, None, None, :]
            expert_out = x[None] + y
            comb = jnp.einsum('bsk,bske->bse', vals, jax.nn.one_hot(idx, E, dtype=x.dtype))
            return jnp.einsum('bse,ebsh->bsh', comb, expert_out)
        key = jax.random.key(seed)
        ks = jax.random.split(key, 4)
        return {'hidden_states': jax.random.normal(ks[0], (B, S, H), jnp.float32), 'router_w': 0.02 * jax.random.normal(ks[1], (L, H, E), jnp.float32), 'router_b': jnp.zeros((L, E), jnp.float32), 'ln_g': jnp.ones((L, E, H), jnp.float32), 'ln_b': jnp.zeros((L, E, H), jnp.float32), 'w1': 0.02 * jax.random.normal(ks[2], (L, E, H, F), jnp.float32), 'b1': jnp.zeros((L, E, F), jnp.float32), 'w2': 0.02 * jax.random.normal(ks[3], (L, E, F, H), jnp.float32), 'b2': jnp.zeros((L, E, H), jnp.float32)}
    _L0_ffn_in = _L0_ffn_setup()
    _d = {'L0_attn_x': _L0_attn_in['x'], 'L0_attn_ln_w': _L0_attn_in['ln_w'], 'L0_attn_ln_b': _L0_attn_in['ln_b'], 'L0_attn_W_in': _L0_attn_in['W_in'], 'L0_attn_conv_w': _L0_attn_in['conv_w'], 'L0_attn_conv_b': _L0_attn_in['conv_b'], 'L0_attn_W_xproj': _L0_attn_in['W_xproj'], 'L0_attn_W_dt': _L0_attn_in['W_dt'], 'L0_attn_b_dt': _L0_attn_in['b_dt'], 'L0_attn_A_log': _L0_attn_in['A_log'], 'L0_attn_D': _L0_attn_in['D'], 'L0_attn_W_out': _L0_attn_in['W_out'], 'L0_ffn_router_w': _L0_ffn_in['router_w'], 'L0_ffn_router_b': _L0_ffn_in['router_b'], 'L0_ffn_ln_g': _L0_ffn_in['ln_g'], 'L0_ffn_ln_b': _L0_ffn_in['ln_b'], 'L0_ffn_w1': _L0_ffn_in['w1'], 'L0_ffn_b1': _L0_ffn_in['b1'], 'L0_ffn_w2': _L0_ffn_in['w2'], 'L0_ffn_b2': _L0_ffn_in['b2']}
    _x0 = _d['L0_attn_x']
    _d['L0_attn_x'] = jax.random.normal(jax.random.fold_in(jax.random.key(seed), 1), (4, 1024, 128), dtype=_x0.dtype)
    del _x0
    return _d

def reference(L0_attn_x, L0_attn_ln_w, L0_attn_ln_b, L0_attn_W_in, L0_attn_conv_w, L0_attn_conv_b, L0_attn_W_xproj, L0_attn_W_dt, L0_attn_b_dt, L0_attn_A_log, L0_attn_D, L0_attn_W_out, L0_ffn_router_w, L0_ffn_router_b, L0_ffn_ln_g, L0_ffn_ln_b, L0_ffn_w1, L0_ffn_b1, L0_ffn_w2, L0_ffn_b2):

    def _L0_attn_ref(x, ln_w, ln_b, W_in, conv_w, conv_b, W_xproj, W_dt, b_dt, A_log, D, W_out):
        import jax, jax.numpy as jnp
        import numpy as np
        B, L, D_MODEL = (4, 256, 128)
        D_INNER = 2 * D_MODEL
        D_STATE = 64
        D_CONV = 4
        DT_RANK = D_MODEL // 16

        def _mamba_block(x, ln_w, ln_b, W_in, conv_w, conv_b, W_xproj, W_dt, b_dt, A_log, D, W_out):
            residual = x
            mu = jnp.mean(x, axis=-1, keepdims=True)
            var = jnp.mean(jnp.square(x - mu), axis=-1, keepdims=True)
            xn = (x - mu) * jax.lax.rsqrt(var + 1e-05) * ln_w + ln_b
            xz = xn @ W_in
            xi, z = jnp.split(xz, 2, axis=-1)
            xc = jnp.transpose(xi, (0, 2, 1))
            xc = jax.lax.conv_general_dilated(xc, conv_w, window_strides=(1,), padding=[(D_CONV - 1, 0)], feature_group_count=D_INNER, dimension_numbers=('NCH', 'OIH', 'NCH'))
            xc = jnp.transpose(xc, (0, 2, 1)) + conv_b
            u = jax.nn.silu(xc)
            x_dbl = u @ W_xproj
            dt_r = x_dbl[..., :DT_RANK]
            Bm = x_dbl[..., DT_RANK:DT_RANK + D_STATE]
            Cm = x_dbl[..., DT_RANK + D_STATE:]
            delta = jax.nn.softplus(dt_r @ W_dt + b_dt)
            A = -jnp.exp(A_log)

            def step(h, inputs):
                d_t, B_t, C_t, u_t = inputs
                dA = jnp.exp(d_t[:, :, None] * A)
                h = h * dA + (d_t * u_t)[:, :, None] * B_t[:, None, :]
                y_t = jnp.einsum('bdn,bn->bd', h, C_t)
                return (h, y_t)
            h0 = jnp.zeros((x.shape[0], D_INNER, D_STATE), x.dtype)
            seq = (jnp.transpose(delta, (1, 0, 2)), jnp.transpose(Bm, (1, 0, 2)), jnp.transpose(Cm, (1, 0, 2)), jnp.transpose(u, (1, 0, 2)))
            _, ys = jax.lax.scan(step, h0, seq)
            y = jnp.transpose(ys, (1, 0, 2)) + u * D
            y = y * jax.nn.silu(z)
            out = y @ W_out
            return residual + out
        return _mamba_block(x, ln_w, ln_b, W_in, conv_w, conv_b, W_xproj, W_dt, b_dt, A_log, D, W_out)

    def _L0_ffn_ref(hidden_states, router_w, router_b, ln_g, ln_b, w1, b1, w2, b2):
        import jax, jax.numpy as jnp
        import numpy as np
        L, E, H, F, K = (4, 4, 128, 512, 2)
        B, S = (4, 256)
        EPS = 1e-05

        def _moe_layer(x, rw, rb, g, b, w1, b1, w2, b2):
            logits = jnp.einsum('bsh,he->bse', x, rw) + rb
            probs = jax.nn.softmax(logits, axis=-1)
            vals, idx = jax.lax.top_k(probs, K)
            vals = vals / vals.sum(axis=-1, keepdims=True)
            mu = x.mean(axis=-1, keepdims=True)
            xc = x - mu
            xhat = xc * jax.lax.rsqrt((xc * xc).mean(axis=-1, keepdims=True) + EPS)
            xe = xhat[None] * g[:, None, None, :] + b[:, None, None, :]
            h = jax.nn.gelu(jnp.einsum('ebsh,ehf->ebsf', xe, w1) + b1[:, None, None, :], approximate=False)
            y = jnp.einsum('ebsf,efh->ebsh', h, w2) + b2[:, None, None, :]
            expert_out = x[None] + y
            comb = jnp.einsum('bsk,bske->bse', vals, jax.nn.one_hot(idx, E, dtype=x.dtype))
            return jnp.einsum('bse,ebsh->bsh', comb, expert_out)
        x = hidden_states
        for l in range(L):
            x = _moe_layer(x, router_w[l], router_b[l], ln_g[l], ln_b[l], w1[l], b1[l], w2[l], b2[l])
        return x
    x = L0_attn_x
    x = _layernorm(x + _L0_attn_ref(x, L0_attn_ln_w, L0_attn_ln_b, L0_attn_W_in, L0_attn_conv_w, L0_attn_conv_b, L0_attn_W_xproj, L0_attn_W_dt, L0_attn_b_dt, L0_attn_A_log, L0_attn_D, L0_attn_W_out), axis=-1)
    x = _layernorm(x + _L0_ffn_ref(x, L0_ffn_router_w, L0_ffn_router_b, L0_ffn_ln_g, L0_ffn_ln_b, L0_ffn_w1, L0_ffn_b1, L0_ffn_w2, L0_ffn_b2), axis=-1)
    return x

_drawn_inputs = setup_inputs


def setup_inputs(seed=0):
    import zlib

    import numpy as np

    out = dict(_drawn_inputs(seed))
    spreads = {'L0_attn_ln_w': (1.0, 0.2),
     'L0_attn_ln_b': (0.0, 0.1),
     'L0_attn_D': (1.0, 0.2),
     'L0_ffn_router_b': (0.0, 0.1),
     'L0_ffn_ln_g': (1.0, 0.6),
     'L0_ffn_ln_b': (0.0, 0.8),
     'L0_ffn_b1': (0.0, 0.437),
     'L0_ffn_b2': (0.0, 0.1)}
    factors = {'L0_attn_conv_b': 24.064,
     'L0_attn_b_dt': 64.0,
     'L0_attn_W_xproj': 8.0,
     'L0_attn_W_dt': 8.0}
    for name, (base, spread) in spreads.items():
        noise = np.random.default_rng([zlib.crc32(name.encode()), seed]).standard_normal(out[name].shape)
        drawn = base * np.exp(spread * noise) if base else spread * noise
        out[name] = jnp.asarray(drawn.astype(out[name].dtype))
    for name, factor in factors.items():
        out[name] = (out[name] * factor).astype(out[name].dtype)
    return out
```

```python
from contextlib import ExitStack

import numpy as np

import concourse.bass as bass
from concourse import mybir

B, L, H = 4, 1024, 128
DI, N, R, KC = 256, 64, 8, 4
NL, E, F = 4, 4, 512
P = 128
HALVES = DI // P
BP = B // 2
TC = 128
NCH = BP * (L // TC)
DB = 128
NBLK = DI // DB
CB = 512 // TC
QD = 2 * CB
NQ = DB // QD
NP = DB // CB
PARTS = 3
RI = 16
ROWS = PARTS * 2 * RI
NRT = NP // RI
CPT = 4
SEG = TC + 1
TS = TC // 64
NT = NCH * TS
TT = 512
EPS = 1e-5
IBLK = 544
GT = 4
NG = NT // GT
SLOTS = NCH // BP + 1


def build(nc, x, vecs, chan, a_log, ident, sel, w_in, w_xproj, w_dt, w_out,
          router_w, router_b, ln_g, ln_b, w1, b1, w2, b2, out):
    fp32 = mybir.dt.float32
    bf16 = mybir.dt.bfloat16
    ALU = mybir.AluOpType
    ACT = mybir.ActivationFunctionType
    AX = mybir.AxisListType

    rows_d = nc.dram_tensor("rows_d", (2, NCH, DI // 64, ROWS, 512), bf16).ap()
    bc_d = nc.dram_tensor("bc_d", (NCH, P, 2, TC), fp32).ap()
    x1_d = nc.dram_tensor("x1_d", (NCH, P, TS, H), fp32).ap()
    u_d = nc.dram_tensor("u_d", (NCH, 2, DI, TC), fp32).ap()
    sz_d = nc.dram_tensor("sz_d", (NCH, 2, DI, TC), fp32).ap()

    ctx = ExitStack()
    with ctx:
        def sb(name, shape, dt=fp32):
            return ctx.enter_context(nc.sbuf_tensor(name, shape, dt))

        def sem(name):
            return ctx.enter_context(nc.semaphore(name))

        PS = ctx.enter_context(nc.psum_tensor("PS", [P, 8, 512], fp32))

        ident_s = sb("ident_s", [P, P])
        selb = sb("selb", [ROWS, RI * P], bf16)
        vecs_s = sb("vecs_s", [P, 2])
        chan_s = sb("chan_s", [P, HALVES, KC + 3])
        A_s = sb("A_s", [P, DI])
        wout_s = sb("wout_s", [P, HALVES, H])
        rw_s = sb("rw_s", [P, NL * E])
        rb_s = sb("rb_s", [P, NL * E])
        g_s = sb("g_s", [P, NL * E])
        lb_s = sb("lb_s", [P, NL * E])
        b1_s = sb("b1_s", [P, NL * E * GT])
        b2_s = sb("b2_s", [E, 2, H])

        carry = sb("carry", [P, SLOTS, DI])

        neg_half = sb("neg_half", [P, 4])
        one = sb("one", [P, 1])

        ARENA = 47800
        arena = sb("arena", [P, ARENA])

        at_ = [0]

        def shaped(v, shape):
            if len(shape) == 2:
                v = v.rearrange("p (a b) -> p a b", b=shape[1])
            elif len(shape) == 3:
                v = v.rearrange("p (a b c) -> p a b c", b=shape[1], c=shape[2])
            elif len(shape) == 4:
                v = v.rearrange("p (a b c d) -> p a b c d", b=shape[1], c=shape[2], d=shape[3])
            return v

        def carve(n):
            at_[0] += n
            assert at_[0] <= ARENA, at_[0]
            return arena[:, at_[0] - n:at_[0]]

        def take(*shape):
            return shaped(carve(int(np.prod(shape))), shape)

        def take_bf16(*shape):
            return shaped(carve(int(np.prod(shape)) // 2).bitcast(bf16), shape)

        at_[0] = 0
        xt = take(4, H)
        xn = take(4, H)
        xnT = take(TT)
        xi = take(2, HALVES, KC - 1 + TT)
        conv = take(HALVES, TT)
        u_s = take(HALVES, TT)
        sz_s = take(HALVES, TT)
        dtr_s = take(TT)
        mag = take(HALVES, TT)
        one_p = take(HALVES, TT)
        slip = take(HALVES, TT)
        lg = take(HALVES, TT)
        rl = take(HALVES, TT)
        dd = take(2, HALVES, TT)
        dl_s, du_s = dd[:, 0], dd[:, 1]
        rest = take(2, HALVES, TT)
        part = [take_bf16(2, HALVES, TT) for _ in range(PARTS)]
        bc_t = take(2, TT)
        sel_t = take(RI * P)
        win_s = take(4 * P)
        wx_s = take(HALVES, R + 2 * N)
        wdt_s = take(DI)
        st_a = take(4, 6)
        mv_a = take(4, 2)
        rs_a = take(4)

        at_[0] = 0
        hb = take(2, DB * SEG)
        dA = take(2, QD * SEG)
        dB = take(2, QD * SEG)
        rows = take_bf16(2, 2 * NRT, 512)
        cd = take(TS * 4, IBLK)
        usz = take(2, HALVES, 2, TC)
        bc = take(2 * 2 * TC)
        xres = take(TS, H)
        G = take(HALVES, TS * P)
        ysb = take(TS, DI)
        xsum = take(TS, H)
        x1c = take(TS, H)
        st_m = take(TS, 6)
        mv_m = take(TS, 2)
        rs_m = take(TS)

        at_[0] = 0
        w1_s = take(2, E, F)
        w1g = take(2, E, F)
        w2_s = take(2, E * GT, H)
        bias1 = take(2, E * GT)
        X = take(NT, H)
        X1 = take(NT, H)
        xTs = take(2, GT * P)
        xg = take(GT, P)
        xhs = take(GT, P)
        xhT = take(2, GT * P)
        hT = take(2, GT, 512)
        lgt = take(GT, E)
        mx = take(GT)
        ex = take(GT, E)
        sm = take(GT)
        pr = take(GT, E)
        rank = take(GT, E)
        order = take(GT, E, E)
        selp = take(GT, E)
        comb = take(2, GT * E)
        csum = take(2, GT)
        combT = take(2, GT * P)
        st_f = take(GT, 6)
        mv_f = take(GT, 2)
        rs_f = take(GT)
        xo = take(2, GT, H)

        passed = sem("passed")
        a_var = sem("a_var")
        a_rs = sem("a_rs")
        p_var = sem("p_var")
        p_rs = sem("p_rs")
        f_var = sem("f_var")
        f_rs = sem("f_rs")
        o_var = sem("o_var")
        o_rs = sem("o_rs")
        weights = sem("weights")
        a_start = sem("a_start")
        zeroed = sem("zeroed")
        prepared = sem("prepared")
        a_x = sem("a_x")
        a_xn = sem("a_xn")
        a_tp = sem("a_tp")
        a_xnT = sem("a_xnT")
        a_xz = sem("a_xz")
        a_xi = sem("a_xi")
        a_pad = sem("a_pad")
        a_conv = sem("a_conv")
        a_u = sem("a_u")
        a_sz = sem("a_sz")
        a_xp = sem("a_xp")
        a_bc = sem("a_bc")
        a_dtr = sem("a_dtr")
        a_v = sem("a_v")
        a_mag = sem("a_mag")
        a_onep = sem("a_onep")
        a_slip = sem("a_slip")
        a_ln = sem("a_ln")
        a_p1 = sem("a_p1")
        a_rest = sem("a_rest")
        a_p2 = sem("a_p2")
        a_p3 = sem("a_p3")
        a_bcs = sem("a_bcs")
        a_delta = sem("a_delta")
        a_du = sem("a_du")
        a_stored = sem("a_stored")
        a_link = sem("a_link")
        a_end = sem("a_end")
        arg_ready = sem("arg_ready")
        du_ready = sem("du_ready")
        exp_done = sem("exp_done")
        mult_done = sem("mult_done")
        scan_done = sem("scan_done")
        slot_ready = sem("slot_ready")
        carried = sem("carried")
        y_done = sem("y_done")
        evacuated = sem("evacuated")
        c_spread = sem("c_spread")
        bc_in = sem("bc_in")
        x1_out = sem("x1_out")
        x_in = sem("x_in")
        post_in = sem("post_in")
        post_t = sem("post_t")
        g_link = sem("g_link")
        g_done = sem("g_done")
        out_ready = sem("out_ready")
        p_link = sem("p_link")
        post_done = sem("post_done")
        f_g = sem("f_g")
        f_bp = sem("f_bp")
        f_bias = sem("f_bias")
        f_xT = sem("f_xT")
        f_xhT = sem("f_xhT")
        f_xTs = sem("f_xTs")
        f_xhTs = sem("f_xhTs")
        f_lg = sem("f_lg")
        f_link = sem("f_link")
        f_rt = sem("f_rt")
        f_cts = sem("f_cts")
        f_h = sem("f_h")
        f_gelu = sem("f_gelu")
        f_y = sem("f_y")
        f_yb = sem("f_yb")
        f_xg = sem("f_xg")
        f_xn = sem("f_xn")
        f_lm = sem("f_lm")
        f_cw = sem("f_cw")
        f_ct = sem("f_ct")
        f_cs = sem("f_cs")
        f_x0 = sem("f_x0")
        f_sum = sem("f_sum")
        f_fin = sem("f_fin")
        f_fl = sem("f_fl")
        rows_in = [sem(f"rows_in{i}") for i in range(2)]
        f_w = [sem(f"f_w{i}") for i in range(2)]
        f_out = [sem(f"f_out{i}") for i in range(2)]

        CARRY0, Y0, EV0, POST0, FIN0, DU0, X0, LG0, XH0 = NBLK, 2, 2, 1, 1, 1, 16, 1, 1
        A_STORES = 2 * HALVES + 2 + 2 * PARTS * (DI // 64)
        F_LOADS = 16 * (E + 2)
        FS0, FY0 = NG * E, 2 * NG * E

        block = ctx.enter_context(nc.Block())

        def run_layers(eng, step):
            with eng.Fori(0, NL // 2) as l2:
                for lp in range(2):
                    l = l2 * 2 + lp
                    step(l2, l, lp, 0, 0, True)
                    with eng.Fori(0, NG // 2 - 1) as g2:
                        for gp in range(2):
                            step(l2, l, lp, g2 * 2 + gp + 1, 1 - gp, True)
                    step(l2, l, lp, NG - 1, 1, False)

        def apart(eng):
            eng.sem_inc(passed, 1)

        def tokens(v, m, s):
            pair, c = m // (NCH // BP), m % (NCH // BP)
            return v[bass.ds(pair * 2, 2), bass.ds(c * TC + s * 64, 64), :].rearrange("b t h -> t b h")

        def seg(v):
            return v.rearrange("p (c s) -> p c s", s=SEG)

        def run_blocks(eng, emit, tail):
            emit(0, 0, 0)
            with eng.Fori(0, NCH - 1) as ch:
                for k in range(1, NBLK + 1):
                    emit(ch, k, 1)
            for k in range(1, NBLK):
                emit(NCH - 1, k, 1)
            tail(NCH - 1)

        @block.sync
        def _(sp):
            for dst, src in ((ident_s[:], ident), (sel_t[0:ROWS, :], sel), (vecs_s[:], vecs),
                             (chan_s[:], chan), (A_s[:], a_log),
                             (win_s, w_in), (wx_s, w_xproj.rearrange("(h p) n -> p h n", p=P)),
                             (wdt_s[0:R, :], w_dt), (wout_s[:], w_out.rearrange("(h p) n -> p h n", p=P)),
                             (rw_s[:], router_w), (rb_s[:], router_b), (g_s[:], ln_g), (lb_s[:], ln_b),
                             (b1_s[:], b1)):
                sp.dma_start(dst, src).then_inc(weights, 16)

            with sp.Fori(0, BP) as bp:
                for k in range(4):
                    n = bp * 4 + k
                    half, bb = k // 2, k % 2
                    sp.wait_ge(a_xn, n + 1)
                    sp.dma_start(xt, x[bp * 2 + bb, half * TT:(half + 1) * TT, :]
                                 .rearrange("(s p) h -> p s h", p=P)).then_inc(a_x, 16)
                    sp.wait_ge(a_sz, n + 1)
                    sp.wait_ge(a_u, n + 1)
                    m0 = bp * 8 + half * CPT
                    for h in range(HALVES):
                        for dram, s in ((u_d, u_s), (sz_d, sz_s)):
                            sp.dma_start(dram[bass.ds(m0, CPT), bb, h * P:(h + 1) * P, :].rearrange("c p t -> p c t"),
                                         s[:, h, :].rearrange("p (c t) -> p c t", c=CPT)).then_inc(a_stored, 16)
                    sp.wait_ge(a_bc, n + 1)
                    q = slice(64 * bb, 64 * bb + N)
                    for i in range(2):
                        sp.dma_start(bc_d[bass.ds(m0, CPT), q, i, :].rearrange("c p t -> p c t"),
                                     bc_t[q, i].rearrange("p (c t) -> p c t", c=CPT)).then_inc(a_stored, 16)
                    sp.wait_ge(a_p3, n + 1)
                    for v in range(2):
                        for w in range(PARTS):
                            for g in range(DI // 64):
                                r0 = w * 2 * RI + bb * RI
                                sp.dma_start(rows_d[v, bass.ds(m0, CPT), g, r0:r0 + RI, :].rearrange(
                                    "c i (j t) -> (i j) c t", t=TC),
                                    part[w][64 * (g % 2):64 * (g % 2) + 64, v, g // 2, :].rearrange(
                                        "p (c t) -> p c t", c=CPT)).then_inc(a_stored, 16)
                    sp.wait_ge(a_stored, (n + 1) * 16 * A_STORES)
                    apart(sp)
            sp.wait_ge(a_end, 3)

            def emit(ch, k, before):
                blk = ch * NBLK + k
                m, kk = ch + k // NBLK, k % NBLK
                if before:
                    sp.wait_ge(du_ready, (blk - 1) * NP + DU0)
                    apart(sp)
                if kk == 0:
                    if before:
                        sp.wait_ge(bc_in, 16 * m)
                        apart(sp)
                    sp.dma_start(bc[:, bass.ds(m % 2 * 2 * TC, 2 * TC)], bc_d[m].rearrange("p i t -> p (i t)")
                                 ).then_inc(bc_in, 16)
                for v in range(2):
                    sp.dma_start(rows[0:ROWS, k % 2, v * NRT:(v + 1) * NRT, :],
                                 rows_d[v, m, kk * NRT:(kk + 1) * NRT].rearrange("g r f -> r g f")
                                 ).then_inc(rows_in[k % 2], 16)
                if kk == 1:
                    sp.wait_ge(post_done, m + POST0)
                    apart(sp)
                    for i, dram in enumerate((u_d, sz_d)):
                        for h in range(HALVES):
                            sp.dma_start(usz[:, i, h, :, :], dram[m, :, h * P:(h + 1) * P, :]
                                         .rearrange("b p t -> p b t")).then_inc(post_in, 16)
                    for s in range(TS):
                        sp.dma_start(xres[:, s, :], tokens(x, m, s)).then_inc(post_in, 16)

            run_blocks(sp, emit, lambda ch: None)

            sp.wait_ge(carried, NCH * NBLK + CARRY0)
            sp.wait_ge(x1_out, 16 * NCH + X0)
            for dst in (X, X1):
                sp.dma_start(dst.rearrange("p (m s) h -> p m (s h)", s=TS),
                             x1_d.rearrange("m p s h -> p m (s h)")).then_inc(x_in, 16)
            sp.wait_ge(post_done, NCH + POST0)
            with sp.Fori(0, NL // 2) as l2:
                for lp in range(2):
                    l = l2 * 2 + lp
                    sp.wait_ge(f_y, NG * E * (l + 1))
                    sp.dma_start(w1_s[:, lp],
                                 w1[l].rearrange("e h f -> h e f")).then_inc(f_w[lp], 16)
                    for e in range(E):
                        sp.dma_start(w2_s[:, lp, e * GT:(e + 1) * GT], w2[l, e].rearrange("(c p) h -> p c h", p=P)
                                     ).then_inc(f_w[lp], 16)
                    sp.dma_start(b2_s[:, lp], b2[l]).then_inc(f_w[lp], 16)
            with sp.Fori(0, NG // 2) as g2:
                for gp in range(2):
                    g = g2 * 2 + gp
                    sp.wait_ge(f_fin, g + 1 + FIN0)
                    apart(sp)
                    for s in range(GT):
                        sp.dma_start(tokens(out, g * (GT // TS) + s // TS, s % TS), xo[:, gp, s, :]
                                     ).then_inc(f_out[gp], 16)
            sp.wait_ge(f_out[0], 8 * NT + 64)
            sp.wait_ge(f_out[1], 8 * NT + 64)

        @block.gpsimd
        def _(pool):
            nc.gpsimd.memset(xi[:, :, :, 0:KC - 1], 0.0).then_inc(a_pad, 1)
            nc.gpsimd.memset(carry[:], 0.0).then_inc(zeroed, 1)
            nc.gpsimd.memset(neg_half[:], -0.5).then_inc(zeroed, 1)
            nc.gpsimd.memset(one[:], 1.0).then_inc(zeroed, 1)
            pool.wait_ge(zeroed, 3)
            ones = one[:].unsqueeze(1).broadcast_to([P, HALVES, TT])

            def rsqrt(rs, asked, answered, count):
                pool.wait_ge(asked, count)
                nc.gpsimd.tensor_tensor(rs, rs, neg_half[:, 0:rs.shape[-1]], ALU.pow).then_inc(answered, 1)
                pool.wait_ge(answered, count)
                apart(pool)

            pool.sem_inc(a_xn, 1)
            pool.sem_inc(carried, CARRY0)
            pool.sem_inc(y_done, Y0)
            pool.sem_inc(evacuated, EV0)
            pool.sem_inc(post_done, POST0)
            pool.sem_inc(du_ready, DU0)
            pool.sem_inc(x1_out, X0)
            pool.sem_inc(post_t, 1)
            pool.sem_inc(f_lg, LG0)
            pool.sem_inc(f_xhT, XH0)
            pool.sem_inc(f_y, FY0)
            pool.sem_inc(f_gelu, 2)
            pool.sem_inc(f_fin, FIN0)
            pool.sem_inc(f_out[0], 64)
            pool.sem_inc(f_out[1], 64)
            with pool.Fori(0, BP) as bp:
                for k in range(4):
                    n = bp * 4 + k
                    rsqrt(rs_a, a_var, a_rs, n + 1)
                    pool.wait_ge(a_mag, 2 * n + 2)
                    nc.gpsimd.tensor_tensor(one_p, mag, ones, ALU.add).then_inc(a_onep, 1)
                    pool.wait_ge(a_onep, n + 1)
                    nc.gpsimd.tensor_tensor(slip, one_p, ones, ALU.subtract).then_inc(a_slip, 1)
                    pool.wait_ge(a_slip, 2 * n + 1)
                    nc.gpsimd.tensor_tensor(slip, slip, mag, ALU.subtract).then_inc(a_slip, 1)
                    pool.wait_ge(a_p1, n + 1)
                    nc.gpsimd.tensor_tensor(rest, dd, part[0], ALU.subtract).then_inc(a_rest, 1)
                    pool.wait_ge(a_p2, n + 1)
                    nc.gpsimd.tensor_tensor(part[2], rest, part[1], ALU.subtract).then_inc(a_p3, 1)
            pool.wait_ge(a_end, 3)
            nc.gpsimd.memset(cd, 0.0).then_inc(zeroed, 1)
            nc.gpsimd.memset(dA, 0.0).then_inc(prepared, 1)
            pool.wait_ge(zeroed, 4)

            def emit(ch, k, before):
                blk = ch * NBLK + k
                m, kk = ch + k // NBLK, k % NBLK
                if k == 1:
                    pool.wait_ge(y_done, blk - 1 + Y0)
                    pool.wait_ge(bc_in, 16 * (ch + 1))
                    pool.wait_ge(carried, blk + CARRY0)
                    for b in range(2):
                        dst = cd[64 * b:64 * b + 64].rearrange("p g (i s) -> p g i s", s=34)[:, :, :, b]
                        src = bc[64 * b:64 * b + 64, bass.ds(m % 2 * 2 * TC + TC, TC)].rearrange(
                            "p (g i) -> p g i", i=16)
                        nc.gpsimd.tensor_copy(dst, src).then_inc(c_spread, 1)
                    pool.wait_ge(c_spread, 2 * ch + 2)
                pool.wait_ge(carried, blk - NBLK + 1 + CARRY0)
                slot = m % (NCH // BP)
                for q in range(NQ):
                    if before or q > 1:
                        pool.wait_ge(scan_done, blk * NQ + q - 1)
                    nc.gpsimd.tensor_copy(seg(dB[:, q % 2])[:, :, 0],
                                          carry[:, slot, kk * DB + q * QD:kk * DB + (q + 1) * QD]
                                          ).then_inc(slot_ready, 1)
                if before and k == NBLK:
                    rsqrt(rs_m, p_var, p_rs, ch + 1)
                pool.wait_ge(scan_done, blk * NQ + NQ)
                nc.gpsimd.tensor_copy(carry[:, slot + 1, kk * DB:(kk + 1) * DB],
                                      seg(hb[:, k % 2])[:, :, TC]).then_inc(carried, 1)

            run_blocks(pool, emit, lambda ch: rsqrt(rs_m, p_var, p_rs, ch + 1))

            def step(l2, l, lp, g, gp, more):
                n = l * NG + g
                if isinstance(g, int) and g == 0:
                    pool.wait_ge(f_w[lp], F_LOADS * (l2 + 1))
                    pool.wait_ge(f_y, NG * E * (l + 1))
                    for e in range(E):
                        nc.gpsimd.tensor_tensor(w1g[:, lp, e], w1_s[:, lp, e],
                                                g_s[:, bass.ds(l * E + e, 1)].broadcast_to([P, F]), ALU.mult).then_inc(f_g, 1)
                    rsqrt(rs_f, f_var, f_rs, n + 1)
                if more:
                    rsqrt(rs_f, f_var, f_rs, n + 2)

            run_layers(pool, step)
            with pool.Fori(0, NG) as g:
                rsqrt(rs_f, o_var, o_rs, g + 1)

        @block.scalar
        def _(act):
            act.wait_ge(weights, 16 * 14)
            nc.scalar.activation(A_s[:], A_s[:], ACT.Exp).then_inc(a_start, 1)
            with act.Fori(0, BP) as bp:
                for k in range(4):
                    n = bp * 4 + k
                    half, bb = k // 2, k % 2
                    act.wait_ge(a_tp, n + 1)
                    nc.scalar.activation(xnT, PS[:, 0, :], ACT.Identity, bias=vecs_s[:, 1:2],
                                         scale=vecs_s[:, 0:1]).then_inc(a_xnT, 1)
                    act.wait_ge(a_xz, 2 * n + 1)
                    nc.scalar.activation(xi[:, bb, :, KC - 1:], PS[:, 1:3, :], ACT.Identity).then_inc(a_xi, 1)
                    act.wait_ge(a_xz, 2 * n + 2)
                    nc.scalar.activation(sz_s, PS[:, 3:5, :], ACT.Silu).then_inc(a_sz, 1)
                    act.wait_ge(a_conv, 2 * n + 1)
                    for h in range(HALVES):
                        last = nc.scalar.activation(u_s[:, h], conv[:, h], ACT.Silu, bias=chan_s[:, h, KC:KC + 1])
                    last.then_inc(a_u, 1)
                    act.wait_ge(a_xp, n + 1)
                    nc.scalar.activation(dtr_s[0:R, :], PS[0:R, 5, :], ACT.Identity).then_inc(a_dtr, 1)
                    act.wait_ge(a_v, n + 1)
                    for h in range(HALVES):
                        last = nc.scalar.activation(mag[:, h], PS[:, 6 + h, :], ACT.Abs,
                                                    bias=chan_s[:, h, KC + 1:KC + 2])
                    last.then_inc(a_mag, 1)
                    act.wait_ge(a_mag, 2 * n + 1)
                    nc.scalar.activation(mag, mag, ACT.Exp, scale=-1.0).then_inc(a_mag, 1)
                    act.wait_ge(a_onep, n + 1)
                    nc.scalar.activation(lg, one_p, ACT.Ln).then_inc(a_ln, 1)
                    act.wait_ge(a_du, n + 1)
                    nc.scalar.activation(part[0], dd, ACT.Identity).then_inc(a_p1, 1)
                    act.wait_ge(a_rest, n + 1)
                    nc.scalar.activation(part[1], rest, ACT.Identity).then_inc(a_p2, 1)
            act.wait_ge(a_ln, 8)
            act.sem_inc(a_end, 1)
            act.wait_ge(prepared, 3)

            def evacuate(ch, k):
                blk1 = ch * NBLK + k - 1
                kk = (k - 1) % NBLK
                act.wait_ge(y_done, blk1 + 1 + Y0)
                if k == 1:
                    act.wait_ge(post_t, ch + 1)
                nc.scalar.activation(ysb[:, :, kk * DB:(kk + 1) * DB],
                                     PS[:, 4 + (k - 1) % 2, 0:TS * DB].rearrange("p (s d) -> p s d", d=DB),
                                     ACT.Identity).then_inc(evacuated, 1)

            def store_x1(ch):
                act.wait_ge(post_done, ch + 1 + POST0)
                act.dma_start(x1_d[ch], x1c).then_inc(x1_out, 16)

            def emit(ch, k, before):
                blk = ch * NBLK + k
                kk = k % NBLK
                for p in range(NP):
                    q = p // 2
                    if p % 2 == 0 and (before or q > 1):
                        act.wait_ge(scan_done, blk * NQ + q - 1)
                    act.wait_ge(arg_ready, blk * NP + p + 1)
                    for j in range(CB):
                        d = kk * DB + CB * p + j
                        c = (p % 2) * CB + j
                        last = nc.scalar.activation(dA[:, q % 2, c * SEG + 1:(c + 1) * SEG],
                                                    PS[:, p % 2, j * TC:(j + 1) * TC], ACT.Exp,
                                                    scale=A_s[:, d:d + 1])
                    last.then_inc(exp_done, 1)
                    if before and p == 14:
                        evacuate(ch, k)
                if before and k == NBLK:
                    store_x1(ch)

            def tail(ch):
                evacuate(ch, NBLK)
                store_x1(ch)

            run_blocks(act, emit, tail)

            def stage_xh(n, gp):
                act.wait_ge(f_xhT, n + 1 + XH0)
                nc.scalar.activation(xhT[:, gp], PS[:, 5, :], ACT.Identity).then_inc(f_xhTs, 1)

            def stage_exp(n):
                act.wait_ge(f_lg, n + 1 + LG0)
                nc.scalar.activation(ex, lgt, ACT.Exp).then_inc(f_rt, 1)

            def step(l2, l, lp, g, gp, more):
                n = l * NG + g
                if g == 0 if isinstance(g, int) else False:
                    stage_xh(n, 0)
                    stage_exp(n)
                    act.wait_ge(f_bias, l + 1)
                for e in range(E):
                    act.wait_ge(f_y, FY0 + E * n + e - 1)
                    for c in range(GT):
                        act.wait_ge(f_h, E * GT * n + GT * e + c + 1)
                        nc.scalar.activation(hT[:, e % 2, c], PS[:, c % 2, :], ACT.Gelu,
                                             bias=bias1[:, lp, e * GT + c:e * GT + c + 1]
                                             ).then_inc(f_gelu, 1)
                    if more and e == 0:
                        stage_xh(n + 1, 1 - gp)
                    if more and e == 1:
                        stage_exp(n + 1)

            run_layers(act, step)

        @block.tensor
        def _(pe):
            pe.wait_ge(weights, 16 * 14)
            with pe.Fori(0, BP) as bp:
                for k in range(4):
                    n = bp * 4 + k
                    half, bb = k // 2, k % 2
                    pe.wait_ge(a_xn, n + 2)
                    for s in range(4):
                        last = nc.tensor.transpose(PS[:, 0, s * P:(s + 1) * P], xn[:, s], ident_s[:])
                    last.then_inc(a_tp, 1)
                    pe.wait_ge(a_xnT, n + 1)
                    for c in range(4):
                        last = nc.tensor.matmul(PS[:, 1 + c, :], win_s[:, c * P:(c + 1) * P], xnT,
                                                start=True, stop=True)
                        if c % 2:
                            last.then_inc(a_xz, 1)
                    pe.wait_ge(a_u, n + 1)
                    for o, lo, hi in ((PS[0:R, 5, :], 0, R), (PS[64 * bb:64 * bb + N, 6, :], R, R + N),
                                      (PS[64 * bb:64 * bb + N, 7, :], R + N, R + 2 * N)):
                        for h in range(HALVES):
                            last = nc.tensor.matmul(o, wx_s[:, h, lo:hi], u_s[:, h], start=(h == 0), stop=(h == 1))
                    last.then_inc(a_xp, 1)
                    pe.wait_ge(a_dtr, n + 1)
                    pe.wait_ge(a_bc, n + 1)
                    for h in range(HALVES):
                        last = nc.tensor.matmul(PS[:, 6 + h, :], wdt_s[0:R, h * P:(h + 1) * P], dtr_s[0:R, :],
                                                start=True, stop=True)
                    last.then_inc(a_v, 1)
            pe.wait_ge(a_v, 8)
            pe.sem_inc(a_end, 1)

            def sum_states(ch, k, part):
                if part == 0:
                    blk = ch * NBLK + k
                    pe.wait_ge(scan_done, blk * NQ)
                    pe.wait_ge(evacuated, blk - 1 - 1 + EV0)
                    if k == 1:
                        pe.wait_ge(c_spread, 2 * ch + 2)
                s, i0 = part // 4, (part % 4) * 4
                for i in range(i0, i0 + 4):
                    for j in range(4):
                        t = s * 64 + j * 16 + i
                        last = nc.tensor.matmul(PS[32 * j:32 * j + 32, 4 + (k - 1) % 2, s * DB:(s + 1) * DB],
                                                cd[:, s * 4 + j, 32 * i:32 * i + 32],
                                                seg(hb[:, (k - 1) % 2])[:, :, 1 + t],
                                                start=(i == 0), stop=(i == 15), tile_position=(0, 32 * j))
                if part == 7:
                    last.then_inc(y_done, 1)

            def turn(ch):
                pe.wait_ge(evacuated, (ch + 1) * NBLK + EV0)
                for h in range(HALVES):
                    for s in range(TS):
                        last = nc.tensor.transpose(PS[:, 6, (h * TS + s) * P:(h * TS + s + 1) * P],
                                                   ysb[:, s, h * P:(h + 1) * P], ident_s[:])
                last.then_inc(post_t, 1)

            def project(ch):
                pe.wait_ge(g_done, ch + 1)
                for s in range(TS):
                    for h in range(HALVES):
                        last = nc.tensor.matmul(PS[:, 7, s * P:(s + 1) * P], G[:, h, s * P:(s + 1) * P],
                                                wout_s[:, h], start=(h == 0), stop=(h == 1))
                last.then_inc(out_ready, 1)

            def emit(ch, k, before):
                blk = ch * NBLK + k
                if before:
                    pe.wait_ge(rows_in[k % 2], 32 * ((ch * NBLK + k) // 2) + 32)
                else:
                    pe.wait_ge(rows_in[0], 32)
                for p in range(NP):
                    if before and p == 18 and k == NBLK:
                        turn(ch)
                    if before and p == 26 and k == NBLK:
                        project(ch)
                    r, g, i = p % 2, p // RI, p % RI
                    pick = selb[:, i * P:(i + 1) * P]
                    if before or p > 1:
                        pe.wait_ge(exp_done, blk * NP + p - 1)
                    nc.tensor.matmul(PS[:, r, :], pick, rows[0:ROWS, k % 2, g, :],
                                     start=True, stop=True).then_inc(arg_ready, 1)
                    if before or p > 1:
                        pe.wait_ge(mult_done, blk * NP + p - 1)
                    nc.tensor.matmul(PS[:, 2 + r, :], pick, rows[0:ROWS, k % 2, NRT + g, :],
                                     start=True, stop=True).then_inc(du_ready, 1)
                    if before and 4 <= p < 12:
                        sum_states(ch, k, p - 4)

            def tail(ch):
                for part in range(8):
                    sum_states(ch, NBLK, part)
                turn(ch)
                project(ch)

            run_blocks(pe, emit, tail)

            def stage_t(n, g):
                pe.wait_ge(f_xg, n + 1)
                pe.wait_ge(f_lg, n + LG0)
                for s in range(GT):
                    last = nc.tensor.transpose(PS[:, 4, s * P:(s + 1) * P], xg[:, s], ident_s[:])
                last.then_inc(f_xT, 1)
                pe.wait_ge(f_xn, n + 1)
                for s in range(GT):
                    last = nc.tensor.transpose(PS[:, 5, s * P:(s + 1) * P], xhs[:, s], ident_s[:])
                last.then_inc(f_xhT, 1)

            def stage_route(n, l, gp):
                pe.wait_ge(f_xTs, n + 1)
                for s in range(GT):
                    last = nc.tensor.matmul(PS[:, 4, s * E:(s + 1) * E], xTs[:, gp, s * P:(s + 1) * P],
                                            rw_s[:, bass.ds(l * E, E)], start=True, stop=True)
                last.then_inc(f_lm, 1)

            def stage_ct(n, gp):
                pe.wait_ge(f_cw, n + 1)
                for s in range(GT):
                    last = nc.tensor.transpose(PS[0:E, 6, s * P:(s + 1) * P], comb[:, gp, s * E:(s + 1) * E],
                                               ident_s[:])
                last.then_inc(f_ct, 1)

            def stage_b2(n, lp, gp):
                pe.wait_ge(f_cts, n + 1)
                for s in range(GT):
                    last = nc.tensor.matmul(PS[:, 7, s * P:(s + 1) * P], combT[0:E, gp, s * P:(s + 1) * P],
                                            b2_s[0:E, lp], start=True, stop=True)
                last.then_inc(f_yb, 1)

            def first(n, lp, gp, e):
                for c in range(GT):
                    i = E * GT * n + GT * e + c
                    pe.wait_ge(f_gelu, i + 1)
                    nc.tensor.matmul(PS[:, c % 2, :], w1g[:, lp, e, c * P:(c + 1) * P], xhT[:, gp],
                                     start=True, stop=True).then_inc(f_h, 1)

            def second(n, lp, e, last_of_layer):
                pe.wait_ge(f_gelu, E * GT * n + GT * e + GT + 2)
                pe.wait_ge(f_sum, FS0 + E * n + e - 1)
                for s in range(GT):
                    for c in range(GT):
                        last = nc.tensor.matmul(PS[:, 2 + e % 2, s * P:(s + 1) * P], hT[:, e % 2, c, s * P:(s + 1) * P],
                                                w2_s[:, lp, e * GT + c], start=(c == 0), stop=(c == GT - 1))
                last.then_inc(f_y, 1)

            def step(l2, l, lp, g, gp, more):
                n = l * NG + g
                if isinstance(g, int) and g == 0:
                    pe.wait_ge(f_w[lp], F_LOADS * (l2 + 1))
                    pe.wait_ge(f_lg, n + LG0)
                    for ec in range(E * GT):
                        e, c = ec // GT, ec % GT
                        last = nc.tensor.matmul(PS[:, 4, ec:ec + 1], w1_s[:, lp, e, c * P:(c + 1) * P],
                                                lb_s[:, bass.ds(l * E + e, 1)], start=True, stop=True)
                    last.then_inc(f_bp, 1)
                    pe.wait_ge(f_bias, l + 1)
                    stage_t(n, 0)
                    stage_route(n, l, 0)
                    stage_ct(n, 0)
                    stage_b2(n, lp, 0)
                    pe.wait_ge(f_g, E * l + E)
                    pe.wait_ge(f_xhTs, n + 1)
                elif not (isinstance(g, int) and g == 0):
                    pe.wait_ge(f_xhTs, n + 1)
                first(n, lp, gp, 0)
                if more:
                    stage_t(n + 1, g + 1)
                first(n, lp, gp, 1)
                second(n, lp, 0, False)
                if more:
                    stage_route(n + 1, l, 1 - gp)
                first(n, lp, gp, 2)
                second(n, lp, 1, False)
                if more:
                    stage_ct(n + 1, 1 - gp)
                first(n, lp, gp, 3)
                second(n, lp, 2, False)
                if more:
                    stage_b2(n + 1, lp, 1 - gp)
                second(n, lp, 3, not more)

            run_layers(pe, step)

        @block.vector
        def _(dve):
            def normalise(link, links, src, st, mv, rs, dst, tiles, asked, answered, count):
                for s in range(tiles):
                    last = nc.vector.bn_stats(st[:, s, :], src(s))
                last.then_inc(link, 1)
                dve.wait_ge(link, links + 1)
                apart(dve)
                for s in range(tiles):
                    last = nc.vector.bn_aggr(mv[:, s, :], st[:, s, :])
                last.then_inc(link, 1)
                dve.wait_ge(link, links + 2)
                nc.vector.tensor_scalar(rs, mv[:, :, 1], EPS, None, ALU.add).then_inc(asked, 1)
                dve.wait_ge(answered, count)
                for s in range(tiles):
                    last = nc.vector.tensor_scalar(dst(s), src(s), mv[:, s, 0:1], rs[:, s:s + 1],
                                                   ALU.subtract, ALU.mult)
                return last

            dve.wait_ge(weights, 16 * 14)
            dve.wait_ge(a_start, 1)
            nc.vector.tensor_scalar(A_s[:], A_s[:], -1.0, None, ALU.mult).then_inc(prepared, 1)
            nc.vector.tensor_copy(selb[:], sel_t[0:ROWS, :]).then_inc(prepared, 1)
            dve.wait_ge(a_pad, 1)
            A_LINKS = 6
            with dve.Fori(0, BP) as bp:
                for k in range(4):
                    n = bp * 4 + k
                    half, bb = k // 2, k % 2
                    dve.wait_ge(a_x, 16 * n + 16)
                    normalise(a_link, n * A_LINKS, lambda s: xt[:, s], st_a, mv_a, rs_a, lambda s: xn[:, s], 4,
                              a_var, a_rs, n + 1).then_inc(a_xn, 1)
                    dve.wait_ge(a_xi, n + 1)
                    for t in range(KC):
                        for h in range(HALVES):
                            tap = chan_s[:, h, t:t + 1]
                            if t == 0:
                                last = nc.vector.tensor_scalar(conv[:, h], xi[:, bb, h, t:t + TT], tap, None, ALU.mult)
                            else:
                                last = nc.vector.scalar_tensor_tensor(conv[:, h], xi[:, bb, h, t:t + TT], tap,
                                                                      conv[:, h], ALU.mult, ALU.add)
                        if t < KC - 1:
                            last.then_inc(a_link, 1)
                            dve.wait_ge(a_link, n * A_LINKS + 3 + t)
                        else:
                            last.then_inc(a_conv, 1)
                    dve.wait_ge(a_conv, 2 * n + 1)
                    pad = xi[:, bb, :, 0:KC - 1]
                    if half == 0:
                        nc.vector.tensor_copy(pad, xi[:, bb, :, TT:]).then_inc(a_conv, 1)
                    else:
                        nc.vector.memset(pad, 0.0).then_inc(a_conv, 1)
                    dve.wait_ge(a_xp, n + 1)
                    for i in range(2):
                        last = nc.vector.tensor_copy(bc_t[64 * bb:64 * bb + N, i], PS[64 * bb:64 * bb + N, 6 + i, :])
                    last.then_inc(a_bc, 1)
                    dve.wait_ge(a_mag, 2 * n + 1)
                    for h in range(HALVES):
                        last = nc.vector.tensor_scalar(rl[:, h], PS[:, 6 + h, :], chan_s[:, h, KC + 1:KC + 2], 0.0,
                                                       ALU.add, ALU.max)
                    dve.wait_ge(a_ln, n + 1)
                    dve.wait_ge(a_slip, 2 * n + 2)
                    nc.vector.tensor_tensor(dl_s, lg, slip, ALU.subtract).then_inc(a_link, 1)
                    dve.wait_ge(a_link, n * A_LINKS + A_LINKS)
                    nc.vector.tensor_tensor(dl_s, dl_s, rl, ALU.add).then_inc(a_delta, 1)
                    dve.wait_ge(a_delta, n + 1)
                    nc.vector.tensor_tensor(du_s, dl_s, u_s, ALU.mult).then_inc(a_du, 1)
            dve.wait_ge(a_du, 8)
            dve.sem_inc(a_end, 1)

            def gate(ch):
                dve.wait_ge(post_in, 96 * ch + 96)
                dve.wait_ge(post_t, ch + 2)
                tok = lambda v: v.rearrange("p b (s t) -> p s t b", s=TS)
                flat = lambda v: v.rearrange("p (s t b) -> p s t b", s=TS, b=2)
                for h in range(HALVES):
                    last = nc.vector.scalar_tensor_tensor(flat(G[:, h]), tok(usz[:, 0, h]),
                                                          chan_s[:, h, KC + 2:KC + 3],
                                                          flat(PS[:, 6, h * TS * P:(h + 1) * TS * P]),
                                                          ALU.mult, ALU.add)
                last.then_inc(g_link, 1)
                dve.wait_ge(g_link, ch + 1)
                for h in range(HALVES):
                    last = nc.vector.tensor_tensor(flat(G[:, h]), flat(G[:, h]), tok(usz[:, 1, h]), ALU.mult)
                last.then_inc(g_done, 1)

            P_LINKS = 3

            def finish_chunk(ch):
                dve.wait_ge(out_ready, ch + 1)
                nc.vector.scalar_tensor_tensor(xsum, xres, 2.0,
                                               PS[:, 7, 0:TS * H].rearrange("p (s h) -> p s h", h=H),
                                               ALU.mult, ALU.add).then_inc(p_link, 1)
                dve.wait_ge(p_link, ch * P_LINKS + 1)
                dve.wait_ge(x1_out, 16 * ch + X0)
                normalise(p_link, ch * P_LINKS + 1, lambda s: xsum[:, s], st_m, mv_m, rs_m, lambda s: x1c[:, s], TS,
                          p_var, p_rs, ch + 1).then_inc(post_done, 1)

            def emit(ch, k, before):
                blk = ch * NBLK + k
                m = ch + k // NBLK
                dve.wait_ge(bc_in, 16 * (m + 1))
                Bc = bc[:, bass.ds(m % 2 * 2 * TC, TC)].unsqueeze(1).broadcast_to([P, CB, TC])
                for q in range(NQ):
                    if before or q > 1:
                        dve.wait_ge(scan_done, blk * NQ + q - 1)
                    for r in range(2):
                        dve.wait_ge(du_ready, blk * NP + 2 * q + r + 1 + DU0)
                        nc.vector.tensor_tensor(seg(dB[:, q % 2])[:, r * CB:(r + 1) * CB, 1:],
                                                PS[:, 2 + r, :].rearrange("p (c t) -> p c t", c=CB), Bc,
                                                ALU.mult).then_inc(mult_done, 1)
                    dve.wait_ge(mult_done, blk * NP + 2 * q + 2)
                    dve.wait_ge(exp_done, blk * NP + 2 * q + 2)
                    dve.wait_ge(slot_ready, blk * NQ + q + 1)
                    if q == 0:
                        dve.wait_ge(y_done, blk - 1 + Y0)
                        dve.wait_ge(carried, blk - 1 + CARRY0)
                    nc.vector.tensor_tensor_scan(hb[:, k % 2, q * QD * SEG:(q + 1) * QD * SEG], dA[:, q % 2],
                                                 dB[:, q % 2], 0.0, ALU.mult, ALU.add).then_inc(scan_done, 1)
                    if before and k == NBLK and q == 10:
                        gate(ch)
                    if before and k == NBLK and q == 14:
                        finish_chunk(ch)

            def tail(ch):
                gate(ch)
                finish_chunk(ch)

            run_blocks(dve, emit, tail)
            dve.wait_ge(carried, NCH * NBLK + CARRY0)

            dve.wait_ge(post_done, NCH + POST0)
            dve.wait_ge(f_w[0], F_LOADS)
            nc.vector.memset(order, 0.0).then_inc(f_sum, FS0)
            dve.wait_ge(f_sum, FS0)
            dve.wait_ge(x_in, 32)

            F_LINKS = 12

            def at(v, g, s):
                return v[:, bass.ds(g * GT + s, 1), :].rearrange("p a h -> p (a h)")

            def stage_norm(n, g):
                dve.wait_ge(f_sum, E * n + E)
                dve.wait_ge(f_xhT, n + XH0)
                nc.vector.tensor_copy(xg, X[:, bass.ds(g * GT, GT), :]).then_inc(f_xg, 1)
                normalise(f_link, n * F_LINKS, lambda s: at(X, g, s), st_f, mv_f, rs_f, lambda s: xhs[:, s], GT,
                          f_var, f_rs, n + 1).then_inc(f_xn, 1)

            def stage_xt(n, gp):
                dve.wait_ge(f_xT, n + 1)
                nc.vector.tensor_copy(xTs[:, gp], PS[:, 4, :]).then_inc(f_xTs, 1)

            def each(v):
                return v.unsqueeze(2).broadcast_to([P, GT, E])

            def stage_router(n, l, gp):
                dve.wait_ge(f_lm, n + 1)
                nc.vector.tensor_tensor(lgt, PS[:, 4, 0:GT * E].rearrange("p (s e) -> p s e", e=E),
                                        rb_s[:, bass.ds(l * E, E)].unsqueeze(1).broadcast_to([P, GT, E]),
                                        ALU.add).then_inc(f_link, 1)
                dve.wait_ge(f_link, n * F_LINKS + 3)
                nc.vector.reduce_max(mx, lgt, AX.X).then_inc(f_link, 1)
                dve.wait_ge(f_link, n * F_LINKS + 4)
                nc.vector.tensor_tensor(lgt, lgt, each(mx), ALU.subtract).then_inc(f_lg, 1)
                dve.wait_ge(f_rt, n + 1)
                nc.vector.reduce_sum(sm, ex, AX.X).then_inc(f_link, 1)
                dve.wait_ge(f_link, n * F_LINKS + 5)
                nc.vector.reciprocal(sm, sm).then_inc(f_link, 1)
                dve.wait_ge(f_link, n * F_LINKS + 6)
                nc.vector.tensor_tensor(pr, ex, each(sm), ALU.mult).then_inc(f_link, 1)
                dve.wait_ge(f_link, n * F_LINKS + 7)
                for j in range(E):
                    pj = pr[:, :, j:j + 1]
                    if j > 0:
                        last = nc.vector.tensor_tensor(order[:, :, j, 0:j], pj.broadcast_to([P, GT, j]),
                                                       pr[:, :, 0:j], ALU.is_gt)
                    if j < E - 1:
                        last = nc.vector.tensor_tensor(order[:, :, j, j + 1:], pj.broadcast_to([P, GT, E - 1 - j]),
                                                       pr[:, :, j + 1:], ALU.is_ge)
                last.then_inc(f_link, 1)
                dve.wait_ge(f_link, n * F_LINKS + 8)
                nc.vector.reduce_sum(rank, order.rearrange("p s j e -> p s e j"), AX.X).then_inc(f_link, 1)
                dve.wait_ge(f_link, n * F_LINKS + 9)
                nc.vector.scalar_tensor_tensor(selp, rank, 2.0, pr, ALU.is_lt, ALU.mult).then_inc(f_link, 1)
                dve.wait_ge(f_link, n * F_LINKS + 10)
                nc.vector.reduce_sum(sm, selp, AX.X).then_inc(f_link, 1)
                dve.wait_ge(f_link, n * F_LINKS + 11)
                nc.vector.reciprocal(sm, sm).then_inc(f_link, 1)
                dve.wait_ge(f_link, n * F_LINKS + 12)
                cw = comb[:, gp].rearrange("p (s e) -> p s e", e=E)
                nc.vector.tensor_tensor(cw, selp, each(sm), ALU.mult).then_inc(f_cw, 1)
                dve.wait_ge(f_cw, n + 1)
                nc.vector.reduce_sum(csum[:, gp], cw, AX.X).then_inc(f_cs, 1)

            def stage_cts(n, gp):
                dve.wait_ge(f_ct, n + 1)
                nc.vector.tensor_copy(combT[0:E, gp], PS[0:E, 6, :]).then_inc(f_cts, 1)

            def start_sum(n, g, gp):
                dve.wait_ge(f_yb, n + 1)
                dve.wait_ge(f_cs, n + 1)
                for s in range(GT):
                    last = nc.vector.scalar_tensor_tensor(at(X, g, s), at(X, g, s), csum[:, gp, s:s + 1],
                                                          PS[:, 7, s * P:(s + 1) * P], ALU.mult, ALU.add)
                last.then_inc(f_x0, 1)

            def add_expert(n, g, gp, e):
                dve.wait_ge(f_y, FY0 + E * n + e + 1)
                dve.wait_ge(f_x0, n + 1)
                dve.wait_ge(f_sum, FS0 + E * n + e)
                for s in range(GT):
                    last = nc.vector.scalar_tensor_tensor(at(X, g, s), PS[:, 2 + e % 2, s * P:(s + 1) * P],
                                                          comb[:, gp, s * E + e:s * E + e + 1], at(X, g, s),
                                                          ALU.mult, ALU.add)
                last.then_inc(f_sum, 1)

            def step(l2, l, lp, g, gp, more):
                n = l * NG + g
                if isinstance(g, int) and g == 0:
                    dve.wait_ge(f_bp, l + 1)
                    nc.vector.tensor_tensor(bias1[:, lp], PS[:, 4, 0:E * GT], b1_s[:, bass.ds(l * E * GT, E * GT)],
                                            ALU.add).then_inc(f_bias, 1)
                    stage_norm(n, 0)
                    stage_xt(n, 0)
                    stage_router(n, l, 0)
                    stage_cts(n, 0)
                if more:
                    stage_norm(n + 1, g + 1)
                start_sum(n, g, gp)
                if more:
                    stage_xt(n + 1, 1 - gp)
                add_expert(n, g, gp, 0)
                if more:
                    stage_router(n + 1, l, 1 - gp)
                add_expert(n, g, gp, 1)
                if more:
                    stage_cts(n + 1, 1 - gp)
                add_expert(n, g, gp, 2)
                add_expert(n, g, gp, 3)

            run_layers(dve, step)

            O_LINKS = 3
            with dve.Fori(0, NG // 2) as g2:
                for gp in range(2):
                    g = g2 * 2 + gp
                    dve.wait_ge(f_sum, FS0 + NG * NL * E)
                    dve.wait_ge(f_fin, g + FIN0)
                    tiles = lambda v: v[:, bass.ds(g * GT, GT), :]
                    nc.vector.tensor_tensor(xhs, tiles(X), tiles(X1), ALU.add).then_inc(f_fl, 1)
                    dve.wait_ge(f_fl, g * O_LINKS + 1)
                    dve.wait_ge(f_out[gp], 64 * g2 + 64)
                    normalise(f_fl, g * O_LINKS + 1, lambda s: xhs[:, s], st_f, mv_f, rs_f, lambda s: xo[:, gp, s], GT,
                              o_var, o_rs, g + 1).then_inc(f_fin, 1)



_INS = ["x", "vecs", "chan", "a_log", "ident", "sel", "w_in", "w_xproj", "w_dt", "w_out",
        "router_w", "router_b", "ln_g", "ln_b", "w1", "b1", "w2", "b2"]


def kernel(L0_attn_x, L0_attn_ln_w, L0_attn_ln_b, L0_attn_W_in, L0_attn_conv_w, L0_attn_conv_b, L0_attn_W_xproj,
           L0_attn_W_dt, L0_attn_b_dt, L0_attn_A_log, L0_attn_D, L0_attn_W_out, L0_ffn_router_w, L0_ffn_router_b,
           L0_ffn_ln_g, L0_ffn_ln_b, L0_ffn_w1, L0_ffn_b1, L0_ffn_w2, L0_ffn_b2):
    import concourse.bacc as bacc
    from concourse.bass_utils import run_bass_kernel_spmd

    f = lambda v: np.asarray(v)
    halves = lambda v: f(v).reshape(HALVES, P).T[:, :, None]
    sel = np.zeros((PARTS, 2, RI, RI, 2, N), np.float32)
    for b in range(2):
        for i in range(RI):
            sel[:, b, i, i, b, :] = 1.0
    data = {
        "x": f(L0_attn_x),
        "vecs": np.stack([f(L0_attn_ln_w), f(L0_attn_ln_b)], 1),
        "chan": np.concatenate([f(L0_attn_conv_w).reshape(HALVES, P, KC).transpose(1, 0, 2), halves(L0_attn_conv_b),
                                halves(L0_attn_b_dt), halves(L0_attn_D)], 2),
        "a_log": np.concatenate([f(L0_attn_A_log).T] * 2, 0),
        "ident": np.eye(P, dtype=np.float32),
        "sel": sel.reshape(ROWS, RI * P),
        "w_in": f(L0_attn_W_in), "w_xproj": f(L0_attn_W_xproj), "w_dt": f(L0_attn_W_dt), "w_out": f(L0_attn_W_out),
        "router_w": f(L0_ffn_router_w).transpose(1, 0, 2).reshape(H, NL * E),
        "router_b": np.concatenate([f(L0_ffn_router_b).reshape(1, NL * E)] * P, 0),
        "ln_g": f(L0_ffn_ln_g).reshape(NL * E, H).T,
        "ln_b": f(L0_ffn_ln_b).reshape(NL * E, H).T,
        "w1": f(L0_ffn_w1),
        "b1": f(L0_ffn_b1).reshape(NL * E * GT, P).T,
        "w2": f(L0_ffn_w2),
        "b2": f(L0_ffn_b2),
    }
    nc = bacc.Bacc("TRN2", target_bir_lowering=False, num_devices=1)
    arrays, args = {}, []
    for name in _INS:
        a = np.ascontiguousarray(data[name])
        arrays[f"in_{name}"] = a
        args.append(nc.dram_tensor(f"in_{name}", a.shape, mybir.dt.from_np(a.dtype), kind="ExternalInput").ap())
    out = nc.dram_tensor("out_dram", (B, L, H), mybir.dt.float32, kind="ExternalOutput").ap()
    build(nc, *args, out)
    r = run_bass_kernel_spmd(nc, [arrays], core_ids=[0])
    return r.results[0]["out_dram"]
```

```python
from contextlib import ExitStack

import numpy as np

import concourse.bass as bass
from concourse import mybir

B, L, H = 4, 1024, 128
DI, N, R, KC = 256, 64, 8, 4
NL, E, F = 4, 4, 512
P = 128
HALVES = DI // P
BP = B // 2
TC = 128
NCH = BP * (L // TC)
DB = 128
NBLK = DI // DB
CB = 512 // TC
QD = 2 * CB
NQ = DB // QD
NP = DB // CB
PARTS = 3
RI = 16
ROWS = PARTS * 2 * RI
NRT = NP // RI
CPT = 4
SEG = TC + 1
TS = TC // 64
NT = NCH * TS
TT = 512
NIT = BP * (L // TT)
EPS = 1e-5
IBLK = 544
GT = 4
NG = NT // GT
SLOTS = NCH // BP + 1


def build(nc, x, vecs, chan, a_log, ident, sel, w_in, w_xproj, w_dt, w_out,
          router_w, router_b, ln_g, ln_b, w1, b1, w2, b2, out):
    fp32 = mybir.dt.float32
    bf16 = mybir.dt.bfloat16
    fp32r = mybir.dt.float32r
    ALU = mybir.AluOpType
    ACT = mybir.ActivationFunctionType
    AX = mybir.AxisListType

    rows_d = nc.dram_tensor("rows_d", (NIT, 2, DI // 64, ROWS, CB, TT), bf16).ap()
    bc_d = nc.dram_tensor("bc_d", (NIT, 2, P, TT), fp32).ap()
    x1_d = nc.dram_tensor("x1_d", (NCH, P, TS, H), fp32).ap()
    u_d = nc.dram_tensor("u_d", (NIT, 2, DI, TT), fp32).ap()
    sz_d = nc.dram_tensor("sz_d", (NIT, 2, DI, TT), fp32).ap()

    ctx = ExitStack()
    with ctx:
        def sb(name, shape, dt=fp32):
            return ctx.enter_context(nc.sbuf_tensor(name, shape, dt))

        def sem(name):
            return ctx.enter_context(nc.semaphore(name))

        PS = ctx.enter_context(nc.psum_tensor("PS", [P, 8, 512], fp32))

        ident_s = sb("ident_s", [P, P])
        selb = sb("selb", [ROWS, RI * P], bf16)
        vecs_s = sb("vecs_s", [P, 2])
        chan_s = sb("chan_s", [P, HALVES, KC + 3])
        A_s = sb("A_s", [P, DI])
        wout_s = sb("wout_s", [P, HALVES, H])
        rw_s = sb("rw_s", [P, NL * E])
        rb_s = sb("rb_s", [P, NL * E])
        g_s = sb("g_s", [P, NL * E])
        lb_s = sb("lb_s", [P, NL * E])
        b1_s = sb("b1_s", [P, NL * E * GT])
        b2_s = sb("b2_s", [E, 2, H])

        carry = sb("carry", [P, SLOTS, DI])

        neg_half = sb("neg_half", [P, 4])
        euler = sb("euler", [P, 1])

        ARENA = 36200
        arena = sb("arena", [P, ARENA])
        BEHIND = 11100
        with nc.sbuf_tensor("behind", [P, BEHIND], fp32) as behind:
            pass
        parts_w1 = sb("parts_w1", [P, 2 * 2 * E * F], fp32r)
        parts_xh = sb("parts_xh", [P, 2 * 2 * GT * P], fp32r)

        at_, space, limit = [0], [arena], [ARENA]

        def shaped(v, shape):
            if len(shape) == 2:
                v = v.rearrange("p (a b) -> p a b", b=shape[1])
            elif len(shape) == 3:
                v = v.rearrange("p (a b c) -> p a b c", b=shape[1], c=shape[2])
            elif len(shape) == 4:
                v = v.rearrange("p (a b c d) -> p a b c d", b=shape[1], c=shape[2], d=shape[3])
            return v

        def carve(n):
            at_[0] += n
            assert at_[0] <= limit[0], at_[0]
            return space[0][:, at_[0] - n:at_[0]]

        def take(*shape):
            return shaped(carve(int(np.prod(shape))), shape)

        def take_bf16(*shape):
            return shaped(carve(int(np.prod(shape)) // 2).bitcast(bf16), shape)

        at_[0] = 0
        xt = take(2, 4, H)
        xn = take(2, 4, H)
        xnT = take(2, TT)
        xi = take(2, HALVES, KC - 1 + TT)
        conv = take(2, HALVES, TT)
        u_s = take(2, HALVES, TT)
        sz_s = take(2, HALVES, TT)
        dtr_s = take(2, TT)
        rest = take(2, 2, HALVES, TT)
        mag, one_p = rest[:, 0], rest[:, 1]
        slip = take(2, HALVES, TT)
        assert at_[0] >= DB * SEG
        part = [[take_bf16(2, HALVES, TT) for _ in range(PARTS)] for _ in range(2)]
        assert at_[0] <= 2 * DB * SEG
        lg = take(2, HALVES, TT)
        rl = take(2, HALVES, TT)
        dd = take(2, 2, HALVES, TT)
        bc_t = take(2, TT)
        win_s = take(4 * P)
        wx_s = take(HALVES, R + 2 * N)
        wdt_s = take(DI)
        st_a = take(2, 4, 6)
        mv_a = take(2, 4, 2)
        rs_a = take(2, 4)

        at_[0] = 0
        hb = take(2, DB * SEG)
        usz = take(2, HALVES, 2, TC)
        xres = take(TS, H)
        G = take(HALVES, TS * P)
        ysb = take(TS, DI)
        xsum = take(TS, H)
        x1c = take(TS, H)
        st_m = take(TS, 6)
        mv_m = take(TS, 2)
        rs_m = take(TS)
        at_[0] = 0
        space[0], limit[0] = behind, BEHIND
        dA = take(2, QD * SEG)
        dB = take(2, QD * SEG)
        rows = take_bf16(2, 2 * NRT, 512)
        bc = take(2 * 2 * TC)
        sel_t = behind[:, at_[0]:at_[0] + RI * P]
        cd = take(TS * 4, IBLK)

        space[0], limit[0] = arena, ARENA
        at_[0] = 0
        w1_s = take(2, E, F)
        w1g = take(2, E, F)
        w1p = parts_w1[:].rearrange("p (l w e f) -> p l w e f", l=2, w=2, e=E)
        xhT = parts_xh[:].rearrange("p (g w t) -> p g w t", g=2, w=2)
        w2_s = take(2, E * GT, H)
        bias1 = take(2, E * GT)
        X = take(NT, H)
        X1 = take(NT, H)
        xTs = take(2, GT * P)
        xg = take(GT, P)
        xhs = take(GT, P)
        hT = take(2, GT, 512)
        lgt = take(GT, E)
        mx = take(GT)
        ex = take(GT, E)
        sm = take(GT)
        pr = take(GT, E)
        rank = take(GT, E)
        order = take(GT, E, E)
        selp = take(GT, E)
        comb = take(2, GT * E)
        csum = take(2, GT)
        combT = take(2, GT * P)
        st_f = take(GT, 6)
        mv_f = take(GT, 2)
        rs_f = take(GT)
        xo = take(2, GT, H)

        passed = sem("passed")
        a_var = sem("a_var")
        a_rs = sem("a_rs")
        p_var = sem("p_var")
        p_rs = sem("p_rs")
        f_var = sem("f_var")
        f_rs = sem("f_rs")
        o_var = sem("o_var")
        o_rs = sem("o_rs")
        weights = sem("weights")
        a_start = sem("a_start")
        zeroed = sem("zeroed")
        prepared = sem("prepared")
        a_x = [sem(f"a_x{i}") for i in range(2)]
        a_xn = sem("a_xn")
        a_tp = sem("a_tp")
        a_xnT = sem("a_xnT")
        a_xip = sem("a_xip")
        a_zp = sem("a_zp")
        a_dtp = sem("a_dtp")
        a_xi = sem("a_xi")
        a_pad = sem("a_pad")
        a_conv = sem("a_conv")
        a_u = sem("a_u")
        a_sz = sem("a_sz")
        a_xp = sem("a_xp")
        a_bc = sem("a_bc")
        a_dtr = sem("a_dtr")
        a_v = sem("a_v")
        a_mag = sem("a_mag")
        a_onep = sem("a_onep")
        a_slip = sem("a_slip")
        a_ln = sem("a_ln")
        a_p1 = sem("a_p1")
        a_rest = sem("a_rest")
        a_p2 = sem("a_p2")
        a_p3 = sem("a_p3")
        a_bcs = sem("a_bcs")
        a_delta = sem("a_delta")
        a_du = sem("a_du")
        a_stored = sem("a_stored")
        a_rows = sem("a_rows")
        a_link = sem("a_link")
        a_tap = sem("a_tap")
        a_rl = sem("a_rl")
        a_exact = sem("a_exact")
        a_end = sem("a_end")
        arg_ready = sem("arg_ready")
        du_ready = sem("du_ready")
        exp_done = sem("exp_done")
        mult_done = sem("mult_done")
        scan_done = sem("scan_done")
        slot_ready = sem("slot_ready")
        carried = sem("carried")
        y_done = sem("y_done")
        evacuated = sem("evacuated")
        c_spread = sem("c_spread")
        bc_in = sem("bc_in")
        x1_out = sem("x1_out")
        x_in = sem("x_in")
        post_in = sem("post_in")
        post_t = sem("post_t")
        g_link = sem("g_link")
        g_done = sem("g_done")
        out_ready = sem("out_ready")
        p_link = sem("p_link")
        post_done = sem("post_done")
        f_g = sem("f_g")
        f_bp = sem("f_bp")
        f_bias = sem("f_bias")
        f_xT = sem("f_xT")
        f_xhT = sem("f_xhT")
        f_xTs = sem("f_xTs")
        f_xhTs = sem("f_xhTs")
        f_lg = sem("f_lg")
        f_link = sem("f_link")
        f_rt = sem("f_rt")
        f_cts = sem("f_cts")
        f_h = sem("f_h")
        f_gelu = sem("f_gelu")
        f_y = sem("f_y")
        f_yb = sem("f_yb")
        f_xg = sem("f_xg")
        f_xhu = sem("f_xhu")
        f_upper = sem("f_upper")
        f_wp = sem("f_wp")
        f_xn = sem("f_xn")
        f_lm = sem("f_lm")
        f_cw = sem("f_cw")
        f_ct = sem("f_ct")
        f_cs = sem("f_cs")
        f_x0 = sem("f_x0")
        f_sum = sem("f_sum")
        f_fin = sem("f_fin")
        f_fl = sem("f_fl")
        rows_in = [sem(f"rows_in{i}") for i in range(2)]
        f_w = [sem(f"f_w{i}") for i in range(2)]
        f_out = [sem(f"f_out{i}") for i in range(2)]

        CARRY0, Y0, EV0, POST0, FIN0, DU0, X0, LG0, XH0 = NBLK, 2, 2, 1, 1, 1, 16, 1, 1
        A_STORES = 2 * (2 + 1)
        ROW_STORES = 2 * PARTS * 2
        F_LOADS = 16 * (E + 2)
        FS0, FY0 = NG * E, 2 * NG * E
        P_LINKS = 3
        HIDDEN = (0, 1, 6)
        LEAD = 0
        P_SUM, SUM_PARTS, P_EVACUATE = 4, 24, 30
        P_TURN, Q_GATE, P_PROJECT, Q_STATS, P_STORE = 1, 2, 11, 6, 22

        block = ctx.enter_context(nc.Block())

        def run_layers(eng, begin, step):
            def layer(at_layer, following):
                step(at_layer, 0, 0, None, True)
                with eng.Fori(0, NG // 2 - 1) as g2:
                    for gp in range(2):
                        step(at_layer, g2 * 2 + gp + 1, 1 - gp, None, True)
                step(at_layer, NG - 1, 1, following, following is not None)

            begin((0, 0, 0))
            layer((0, 0, 0), (1, 0, 1))
            with eng.Fori(1, NL // 2) as l2:
                layer((l2 * 2 - 1, l2 - 1, 1), (l2 * 2, l2, 0))
                layer((l2 * 2, l2, 0), (l2 * 2 + 1, l2, 1))
            layer((NL - 1, NL // 2 - 1, 1), None)

        def apart(eng):
            eng.sem_inc(passed, 1)

        def tokens(v, m, s):
            pair, c = m // (NCH // BP), m % (NCH // BP)
            return v[bass.ds(pair * 2, 2), bass.ds(c * TC + s * 64, 64), :].rearrange("b t h -> t b h")

        def load_bc(eng, m):
            for b in range(2):
                eng.dma_start(bc[N * b:N * b + N, bass.ds(m % 2 * 2 * TC, 2 * TC)].rearrange("n (i t) -> n i t", t=TC),
                              bc_d[m // CPT, b, :, bass.ds(m % CPT * TC, TC)].rearrange("(i n) t -> n i t", n=N)
                              ).then_inc(bc_in, 16)

        def load_rows(eng, m, kk):
            for v in range(2):
                for g in range(NRT):
                    eng.dma_start(rows[0:ROWS, kk, v * NRT + g, :].rearrange("r (j t) -> r j t", t=TC),
                                  rows_d[m // CPT, v, kk * NRT + g, :, :, bass.ds(m % CPT * TC, TC)]
                                  ).then_inc(rows_in[kk], 16)

        def seg(v):
            return v.rearrange("p (c s) -> p c s", s=SEG)

        def run_blocks(eng, emit, tail):
            emit(0, 0, 0, 0)
            for kk in range(1, NBLK):
                emit(0, kk, 1, 0)
            with eng.Fori(1, NCH) as m:
                for kk in range(NBLK):
                    emit(m, kk, 1, int(kk == 1))
            tail(NCH - 1)

        @block.sync
        def _(sp):
            for dst, src in ((ident_s[:], ident), (sel_t[0:ROWS, :], sel), (vecs_s[:], vecs),
                             (chan_s[:], chan), (A_s[:], a_log),
                             (win_s, w_in), (wx_s, w_xproj.rearrange("(h p) n -> p h n", p=P)),
                             (wdt_s[0:R, :], w_dt), (wout_s[:], w_out.rearrange("(h p) n -> p h n", p=P)),
                             (rw_s[:], router_w), (rb_s[:], router_b), (g_s[:], ln_g), (lb_s[:], ln_b),
                             (b1_s[:], b1)):
                sp.dma_start(dst, src).then_inc(weights, 16)

            def load_x(pair, half, bb):
                sp.dma_start(xt[:, bb], x[bass.ds(pair * 2 + bb, 1), half * TT:(half + 1) * TT, :]
                             .rearrange("b (s p) h -> p (b s) h", p=P)).then_inc(a_x[bb], 16)

            for bb in range(2):
                load_x(0, 0, bb)
            with sp.Fori(0, BP) as bp:
                for half in range(2):
                    it = bp * 2 + half
                    m0 = bp * 8 + half * CPT
                    for bb in range(2):
                        sp.wait_ge(a_xn, 2 * it + bb + 1)
                        load_x((bp + half) % BP, 1 - half, bb)
                    for bb in range(2):
                        sp.wait_ge(a_sz, 2 * it + bb + 1)
                        sp.wait_ge(a_u, 2 * it + bb + 1)
                        apart(sp)
                        for dram, s in ((u_d, u_s), (sz_d, sz_s)):
                            sp.dma_start(dram[it, bb].rearrange("(h p) t -> p h t", p=P), s[:, bb]
                                         ).then_inc(a_stored, 16)
                    for bb in range(2):
                        sp.wait_ge(a_bc, 2 * it + bb + 1)
                        apart(sp)
                        sp.dma_start(bc_d[it, bb], bc_t[:, bb]).then_inc(a_stored, 16)
                    for bb in range(2):
                        sp.wait_ge(a_p3, 2 * it + bb + 3)
                        apart(sp)
                        for w in range(PARTS):
                            for gl in range(2):
                                r0 = w * 2 * RI + bb * RI
                                sp.dma_start(
                                    rows_d[it].rearrange("v (gh gl) r j t -> gl r j (v gh) t", gl=2)
                                    [gl, r0:r0 + RI].rearrange("i j q t -> (i j) q t"),
                                    part[bb][w][64 * gl:64 * gl + 64].rearrange("p v h t -> p (v h) t")
                                    ).then_inc(a_rows, 16)
            for bb in range(2):
                sp.wait_ge(a_x[bb], 16 * NIT + 16)
            sp.wait_ge(a_stored, NIT * 16 * A_STORES + 16)
            sp.sem_inc(a_end, 1)
            sp.wait_ge(a_end, 4)
            sp.wait_ge(a_rows, NIT * 16 * ROW_STORES + 16)

            def emit(m, kk, before, post):
                blk = m * NBLK + kk
                if before:
                    sp.wait_ge(du_ready, (blk - 1) * NP + DU0)
                    apart(sp)
                    if kk == 0:
                        sp.wait_ge(bc_in, 32 * m)
                        apart(sp)
                        load_bc(sp, m)
                    load_rows(sp, m, kk)
                if kk == 1:
                    sp.wait_ge(post_done, m + POST0)
                    apart(sp)
                    for i, dram in enumerate((u_d, sz_d)):
                        for h in range(HALVES):
                            sp.dma_start(usz[:, i, h, :, :], dram[m // CPT, :, h * P:(h + 1) * P,
                                                                  bass.ds(m % CPT * TC, TC)]
                                         .rearrange("b p t -> p b t")).then_inc(post_in, 16)
                    for s in range(TS):
                        sp.dma_start(xres[:, s, :], tokens(x, m, s)).then_inc(post_in, 16)

            run_blocks(sp, emit, lambda m: None)

            sp.wait_ge(carried, NCH * NBLK + CARRY0)
            sp.wait_ge(x1_out, 16 * NCH + X0)
            for dst in (X, X1):
                sp.dma_start(dst.rearrange("p (m s) h -> p m (s h)", s=TS),
                             x1_d.rearrange("m p s h -> p m (s h)")).then_inc(x_in, 16)
            sp.wait_ge(post_done, NCH + POST0)
            with sp.Fori(0, NL // 2) as l2:
                for lp in range(2):
                    l = l2 * 2 + lp
                    sp.wait_ge(f_y, NG * E * (l + 1))
                    sp.dma_start(w1_s[:, lp],
                                 w1[l].rearrange("e h f -> h e f")).then_inc(f_w[lp], 16)
                    for e in range(E):
                        sp.dma_start(w2_s[:, lp, e * GT:(e + 1) * GT], w2[l, e].rearrange("(c p) h -> p c h", p=P)
                                     ).then_inc(f_w[lp], 16)
                    sp.dma_start(b2_s[:, lp], b2[l]).then_inc(f_w[lp], 16)
            with sp.Fori(0, NG // 2) as g2:
                for gp in range(2):
                    g = g2 * 2 + gp
                    sp.wait_ge(f_fin, g + 1 + FIN0)
                    apart(sp)
                    for s in range(GT):
                        sp.dma_start(tokens(out, g * (GT // TS) + s // TS, s % TS), xo[:, gp, s, :]
                                     ).then_inc(f_out[gp], 16)
            sp.wait_ge(f_out[0], 8 * NT + 64)
            sp.wait_ge(f_out[1], 8 * NT + 64)

        @block.gpsimd
        def _(pool):
            nc.gpsimd.memset(xi[:, :, :, 0:KC - 1], 0.0).then_inc(a_pad, 1)
            nc.gpsimd.memset(carry[:], 0.0).then_inc(zeroed, 1)
            nc.gpsimd.memset(neg_half[:], -0.5).then_inc(zeroed, 1)
            nc.gpsimd.memset(euler[:], float(np.e)).then_inc(zeroed, 1)
            pool.wait_ge(zeroed, 3)

            def rsqrt(rs, asked, answered, count):
                pool.wait_ge(asked, count)
                nc.gpsimd.tensor_tensor(rs, rs, neg_half[:, 0:rs.shape[-1]], ALU.pow).then_inc(answered, 1)
                pool.wait_ge(answered, count)
                apart(pool)

            nc.gpsimd.memset(dA, 0.0).then_inc(prepared, 1)
            pool.wait_ge(prepared, 3)
            nc.gpsimd.memset(cd, 0.0).then_inc(zeroed, 1)
            pool.wait_ge(zeroed, 4)

            pool.sem_inc(a_stored, 16)
            pool.sem_inc(a_rows, 16)
            pool.sem_inc(a_p3, 2)
            pool.sem_inc(carried, CARRY0)
            pool.sem_inc(y_done, Y0)
            pool.sem_inc(evacuated, EV0)
            pool.sem_inc(post_done, POST0)
            pool.sem_inc(du_ready, DU0)
            pool.sem_inc(x1_out, X0)
            pool.sem_inc(post_t, 1)
            pool.sem_inc(f_lg, LG0)
            pool.sem_inc(f_xhT, XH0)
            pool.sem_inc(f_y, FY0)
            pool.sem_inc(f_gelu, 3)
            pool.sem_inc(f_fin, FIN0)
            pool.sem_inc(f_out[0], 64)
            pool.sem_inc(f_out[1], 64)
            with pool.Fori(0, BP) as bp:
                for half in range(2):
                    it = bp * 2 + half
                    for bb in range(2):
                        rsqrt(rs_a[:, bb], a_var, a_rs, 2 * it + bb + 1)
                    for bb in range(2):
                        pool.wait_ge(a_p1, 2 * it + bb + 1)
                        nc.gpsimd.tensor_tensor(rest[:, bb], dd[:, bb], part[bb][0], ALU.subtract).then_inc(a_rest, 1)
                    for bb in range(2):
                        pool.wait_ge(a_p2, 2 * it + bb + 1)
                        nc.gpsimd.tensor_tensor(part[bb][2], rest[:, bb], part[bb][1], ALU.subtract).then_inc(a_p3, 1)
            pool.wait_ge(a_p3, 2 * NIT + 2)
            pool.wait_ge(a_end, 4)
            def emit(m, kk, before, post):
                blk = m * NBLK + kk
                if kk == 1:
                    pool.wait_ge(y_done, blk - 1 + Y0)
                    pool.wait_ge(bc_in, 32 * (m + 1))
                    pool.wait_ge(carried, blk + CARRY0)
                    for b in range(2):
                        dst = cd[64 * b:64 * b + 64].rearrange("p g (i s) -> p g i s", s=34)[:, :, :, b]
                        src = bc[64 * b:64 * b + 64, bass.ds(m % 2 * 2 * TC + TC, TC)].rearrange(
                            "p (g i) -> p g i", i=16)
                        nc.gpsimd.tensor_copy(dst, src).then_inc(c_spread, 1)
                    pool.wait_ge(c_spread, 2 * m + 2)
                pool.wait_ge(carried, blk - NBLK + 1 + CARRY0)
                slot = m % (NCH // BP)
                for q in range(NQ):
                    if before or q > 1:
                        pool.wait_ge(scan_done, blk * NQ + q - 1)
                    nc.gpsimd.tensor_copy(seg(dB[:, q % 2])[:, :, 0],
                                          carry[:, slot, kk * DB + q * QD:kk * DB + (q + 1) * QD]
                                          ).then_inc(slot_ready, 1)
                    if post and q == Q_STATS + 2:
                        rsqrt(rs_m, p_var, p_rs, m)
                pool.wait_ge(scan_done, blk * NQ + NQ)
                nc.gpsimd.tensor_copy(carry[:, slot + 1, kk * DB:(kk + 1) * DB],
                                      seg(hb[:, kk])[:, :, TC]).then_inc(carried, 1)

            run_blocks(pool, emit, lambda m: rsqrt(rs_m, p_var, p_rs, m + 1))

            def stage_exp(n):
                pool.wait_ge(f_lg, n + 1 + LG0)
                nc.gpsimd.tensor_tensor(ex, euler[:].unsqueeze(2).broadcast_to([P, GT, E]), lgt, ALU.pow
                                        ).then_inc(f_rt, 1)

            def prepare(l, pair, lp):
                pool.wait_ge(f_w[lp], F_LOADS * (pair + 1))
                pool.wait_ge(f_y, NG * E * (l + 1))
                for e in range(E):
                    nc.gpsimd.tensor_tensor(w1g[:, lp, e], w1_s[:, lp, e],
                                            g_s[:, bass.ds(l * E + e, 1)].broadcast_to([P, F]), ALU.mult
                                            ).then_inc(f_g, 1)

            def begin(first_layer):
                prepare(*first_layer)
                rsqrt(rs_f, f_var, f_rs, 1)
                stage_exp(0)

            def step(layer, g, gp, new, more):
                n = layer[0] * NG + g
                if more:
                    rsqrt(rs_f, f_var, f_rs, n + 2)
                if new:
                    prepare(*new)
                if more:
                    stage_exp(n + 1)

            run_layers(pool, begin, step)
            with pool.Fori(0, NG) as g:
                rsqrt(rs_f, o_var, o_rs, g + 1)

        @block.scalar
        def _(act):
            act.wait_ge(weights, 16 * 14)
            nc.scalar.activation(A_s[:], A_s[:], ACT.Exp).then_inc(a_start, 1)
            with act.Fori(0, BP) as bp:
                for half in range(2):
                    it = bp * 2 + half
                    for bb in range(2):
                        act.wait_ge(a_tp, 2 * it + bb + 1)
                        nc.scalar.activation(xnT[:, bb], PS[:, 4 * bb + 3, :], ACT.Identity, bias=vecs_s[:, 1:2],
                                             scale=vecs_s[:, 0:1]).then_inc(a_xnT, 1)
                    for bb in range(2):
                        act.wait_ge(a_xip, 2 * it + bb + 1)
                        nc.scalar.activation(xi[:, bb, :, KC - 1:], PS[:, 4 * bb:4 * bb + 2, :], ACT.Identity
                                             ).then_inc(a_xi, 1)
                    act.wait_ge(a_stored, it * 16 * A_STORES + 16)
                    for bb in range(2):
                        act.wait_ge(a_zp, 2 * it + bb + 1)
                        nc.scalar.activation(sz_s[:, bb], PS[:, 4 * bb + 2:4 * bb + 4, :], ACT.Silu).then_inc(a_sz, 1)
                    for bb in range(2):
                        act.wait_ge(a_conv, 2 * (2 * it + bb) + 1)
                        for h in range(HALVES):
                            last = nc.scalar.activation(u_s[:, bb, h], conv[:, bb, h], ACT.Silu,
                                                        bias=chan_s[:, h, KC:KC + 1])
                        last.then_inc(a_u, 1)
                    for bb in range(2):
                        act.wait_ge(a_dtp, 2 * it + bb + 1)
                        nc.scalar.activation(dtr_s[0:R, bb, :], PS[0:R, 4 * bb, :], ACT.Identity).then_inc(a_dtr, 1)
                    act.wait_ge(a_p3, 2 * it + 2)
                    for bb in range(2):
                        act.wait_ge(a_v, 2 * it + bb + 1)
                        for h in range(HALVES):
                            last = nc.scalar.activation(mag[:, bb, h], PS[:, 4 * bb + 2 + h, :], ACT.Abs,
                                                        bias=chan_s[:, h, KC + 1:KC + 2])
                        last.then_inc(a_mag, 1)
                    for bb in range(2):
                        act.wait_ge(a_mag, 4 * it + 2 + bb)
                        nc.scalar.activation(mag[:, bb], mag[:, bb], ACT.Exp, scale=-1.0).then_inc(a_mag, 1)
                    for bb in range(2):
                        act.wait_ge(a_onep, 2 * it + bb + 1)
                        nc.scalar.activation(lg[:, bb], one_p[:, bb], ACT.Ln).then_inc(a_ln, 1)
                    act.wait_ge(a_rows, it * 16 * ROW_STORES + 16)
                    for bb in range(2):
                        act.wait_ge(a_du, 2 * it + bb + 1)
                        nc.scalar.activation(part[bb][0], dd[:, bb], ACT.Identity).then_inc(a_p1, 1)
                    for bb in range(2):
                        act.wait_ge(a_rest, 2 * it + bb + 1)
                        nc.scalar.activation(part[bb][1], rest[:, bb], ACT.Identity).then_inc(a_p2, 1)
            load_bc(act, 0)
            load_rows(act, 0, 0)
            act.wait_ge(a_ln, 2 * NIT)
            act.sem_inc(a_end, 1)
            act.wait_ge(prepared, 3)

            def evacuate(m, kk):
                act.wait_ge(y_done, m * NBLK + kk + 1 + Y0)
                if kk == 0:
                    act.wait_ge(post_t, m + 1)
                nc.scalar.activation(ysb[:, :, kk * DB:(kk + 1) * DB],
                                     PS[:, 4 + kk, 0:TS * DB].rearrange("p (s d) -> p s d", d=DB),
                                     ACT.Identity).then_inc(evacuated, 1)

            def store_x1(m):
                act.wait_ge(post_done, m + 1 + POST0)
                act.dma_start(x1_d[m], x1c).then_inc(x1_out, 16)

            def emit(m, kk, before, post):
                blk = m * NBLK + kk
                for p in range(NP):
                    q = p // 2
                    if p % 2 == 0 and (before or q > 1):
                        act.wait_ge(scan_done, blk * NQ + q - 1)
                    act.wait_ge(arg_ready, blk * NP + p + 1)
                    for j in range(CB):
                        d = kk * DB + CB * p + j
                        c = (p % 2) * CB + j
                        last = nc.scalar.activation(dA[:, q % 2, c * SEG + 1:(c + 1) * SEG],
                                                    PS[:, p % 2, j * TC:(j + 1) * TC], ACT.Exp,
                                                    scale=A_s[:, d:d + 1])
                    last.then_inc(exp_done, 1)
                    if before and p == P_EVACUATE:
                        evacuate(m if kk else m - 1, 1 - kk)
                    if post and p == P_STORE:
                        store_x1(m - 1)

            def tail(m):
                evacuate(m, NBLK - 1)
                store_x1(m)

            run_blocks(act, emit, tail)

            def step(layer, g, gp, new, more):
                l, pair, lp = layer
                n = l * NG + g
                if isinstance(g, int) and g == 0:
                    act.wait_ge(f_bias, l + 1)
                for e in range(E):
                    act.wait_ge(f_y, FY0 + E * n + e - 1)
                    for c in range(GT):
                        act.wait_ge(f_h, E * GT * n + GT * e + c + 1)
                        nc.scalar.activation(hT[:, e % 2, c], PS[:, HIDDEN[(GT * e + c) % 3], :], ACT.Gelu,
                                             bias=bias1[:, lp, e * GT + c:e * GT + c + 1]
                                             ).then_inc(f_gelu, 1)

            run_layers(act, lambda first_layer: None, step)

        @block.tensor
        def _(pe):
            pe.wait_ge(weights, 16 * 14)
            with pe.Fori(0, BP) as bp:
                for half in range(2):
                    it = bp * 2 + half
                    for bb in range(2):
                        pe.wait_ge(a_xn, 2 * it + bb + 1)
                        for s in range(4):
                            last = nc.tensor.transpose(PS[:, 4 * bb + 3, s * P:(s + 1) * P], xn[:, bb, s], ident_s[:])
                        last.then_inc(a_tp, 1)
                    for bb in range(2):
                        pe.wait_ge(a_xnT, 2 * it + bb + 1)
                        for c in range(2):
                            last = nc.tensor.matmul(PS[:, 4 * bb + c, :], win_s[:, c * P:(c + 1) * P], xnT[:, bb],
                                                    start=True, stop=True)
                        last.then_inc(a_xip, 1)
                    for bb in range(2):
                        for c in range(2, 4):
                            last = nc.tensor.matmul(PS[:, 4 * bb + c, :], win_s[:, c * P:(c + 1) * P], xnT[:, bb],
                                                    start=True, stop=True)
                        last.then_inc(a_zp, 1)
                    for bb in range(2):
                        pe.wait_ge(a_u, 2 * it + bb + 1)
                        for h in range(HALVES):
                            last = nc.tensor.matmul(PS[0:R, 4 * bb, :], wx_s[:, h, 0:R], u_s[:, bb, h],
                                                    start=(h == 0), stop=(h == 1))
                        last.then_inc(a_dtp, 1)
                        for h in range(HALVES):
                            last = nc.tensor.matmul(PS[:, 4 * bb + 1, :], wx_s[:, h, R:], u_s[:, bb, h],
                                                    start=(h == 0), stop=(h == 1))
                        last.then_inc(a_xp, 1)
                    for bb in range(2):
                        pe.wait_ge(a_dtr, 2 * it + bb + 1)
                        pe.wait_ge(a_sz, 2 * it + bb + 1)
                        for h in range(HALVES):
                            last = nc.tensor.matmul(PS[:, 4 * bb + 2 + h, :], wdt_s[0:R, h * P:(h + 1) * P],
                                                    dtr_s[0:R, bb, :], start=True, stop=True)
                        last.then_inc(a_v, 1)
            pe.wait_ge(a_v, 8)
            pe.sem_inc(a_end, 1)

            def sum_states(m, kk, part):
                if part == 0:
                    blk = m * NBLK + kk
                    pe.wait_ge(scan_done, (blk + 1) * NQ)
                    pe.wait_ge(evacuated, blk - 1 + EV0)
                    if kk == 0:
                        pe.wait_ge(c_spread, 2 * m + 2)
                for step in range(part * TC // SUM_PARTS, (part + 1) * TC // SUM_PARTS):
                    s, i, j = step // 64, step % 64 // 4, step % 4
                    t = s * 64 + j * 16 + i
                    last = nc.tensor.matmul(PS[32 * j:32 * j + 32, 4 + kk, s * DB:(s + 1) * DB],
                                            cd[:, s * 4 + j, 32 * i:32 * i + 32], seg(hb[:, kk])[:, :, 1 + t],
                                            start=(i == 0), stop=(i == 15), tile_position=(0, 32 * j))
                if part == SUM_PARTS - 1:
                    last.then_inc(y_done, 1)

            def turn(m):
                pe.wait_ge(evacuated, (m + 1) * NBLK + EV0)
                for h in range(HALVES):
                    for s in range(TS):
                        last = nc.tensor.transpose(PS[:, 6, (h * TS + s) * P:(h * TS + s + 1) * P],
                                                   ysb[:, s, h * P:(h + 1) * P], ident_s[:])
                last.then_inc(post_t, 1)

            def project(m):
                pe.wait_ge(g_done, m + 1)
                for s in range(TS):
                    for h in range(HALVES):
                        last = nc.tensor.matmul(PS[:, 7, s * P:(s + 1) * P], G[:, h, s * P:(s + 1) * P],
                                                wout_s[:, h], start=(h == 0), stop=(h == 1))
                last.then_inc(out_ready, 1)

            def spread_delta(blk, kk, p, reused):
                if reused:
                    pe.wait_ge(exp_done, blk * NP + p - 1)
                i, g = p % RI, p // RI
                nc.tensor.matmul(PS[:, p % 2, :], selb[:, i * P:(i + 1) * P], rows[0:ROWS, kk, g, :],
                                 start=True, stop=True).then_inc(arg_ready, 1)

            def spread_du(blk, kk, p, reused):
                if reused:
                    pe.wait_ge(mult_done, blk * NP + p - 1)
                i, g = p % RI, p // RI
                nc.tensor.matmul(PS[:, 2 + p % 2, :], selb[:, i * P:(i + 1) * P], rows[0:ROWS, kk, NRT + g, :],
                                 start=True, stop=True).then_inc(du_ready, 1)

            def emit(m, kk, before, post):
                blk = m * NBLK + kk
                pe.wait_ge(rows_in[kk], 64 * m + 64)
                for p in range(NP):
                    spread_delta(blk, kk, p, before or p > 1)
                    if p >= LEAD:
                        spread_du(blk, kk, p - LEAD, before or p - LEAD > 1)
                    elif before:
                        spread_du(blk - 1, 1 - kk, NP + p - LEAD, 1)
                    if post and p == P_TURN:
                        turn(m - 1)
                    if post and p == P_PROJECT:
                        project(m - 1)
                    if before and 0 <= p - P_SUM < SUM_PARTS:
                        sum_states(m if kk else m - 1, 1 - kk, p - P_SUM)

            def tail(m):
                for p in range(NP - LEAD, NP):
                    spread_du(m * NBLK + NBLK - 1, NBLK - 1, p, 1)
                for part in range(SUM_PARTS):
                    sum_states(m, NBLK - 1, part)
                turn(m)
                project(m)

            run_blocks(pe, emit, tail)

            def stage_xt(n):
                pe.wait_ge(f_xg, n + 1)
                pe.wait_ge(f_lg, n + LG0)
                for s in range(GT):
                    last = nc.tensor.transpose(PS[:, 4, s * P:(s + 1) * P], xg[:, s], ident_s[:])
                last.then_inc(f_xT, 1)

            def stage_xh(n):
                pe.wait_ge(f_xn, n + 1)
                for s in range(GT):
                    last = nc.tensor.transpose(PS[:, 5, s * P:(s + 1) * P], xhs[:, s], ident_s[:])
                last.then_inc(f_xhT, 1)

            def stage_route(n, l, gp):
                pe.wait_ge(f_xTs, n + 1)
                for s in range(GT):
                    last = nc.tensor.matmul(PS[:, 4, s * E:(s + 1) * E], xTs[:, gp, s * P:(s + 1) * P],
                                            rw_s[:, bass.ds(l * E, E)], start=True, stop=True)
                last.then_inc(f_lm, 1)

            def stage_ct(n, gp):
                pe.wait_ge(f_cw, n + 1)
                for s in range(GT):
                    last = nc.tensor.transpose(PS[0:E, 5, s * P:(s + 1) * P], comb[:, gp, s * E:(s + 1) * E],
                                               ident_s[:])
                last.then_inc(f_ct, 1)

            def stage_b2(n, lp, gp):
                pe.wait_ge(f_cts, n + 1)
                for s in range(GT):
                    last = nc.tensor.matmul(PS[:, 7, s * P:(s + 1) * P], combT[0:E, gp, s * P:(s + 1) * P],
                                            b2_s[0:E, lp], start=True, stop=True)
                last.then_inc(f_yb, 1)

            def bias_of_offset(l, pair, lp):
                pe.wait_ge(f_w[lp], F_LOADS * (pair + 1))
                for ec in range(E * GT):
                    e, c = ec // GT, ec % GT
                    last = nc.tensor.matmul(PS[:, 4, ec:ec + 1], w1_s[:, lp, e, c * P:(c + 1) * P],
                                            lb_s[:, bass.ds(l * E + e, 1)], start=True, stop=True)
                last.then_inc(f_bp, 1)
                pe.wait_ge(f_bias, l + 1)

            def first(n, lp, gp, e):
                for c in range(GT):
                    i = E * GT * n + GT * e + c
                    pe.wait_ge(f_gelu, i + (3 if e == c == 0 else 1))
                    for part_w, part_x in ((0, 0), (0, 1), (1, 0)):
                        last = nc.tensor.matmul(PS[:, HIDDEN[(GT * e + c) % 3], :],
                                                w1p[:, lp, part_w, e, c * P:(c + 1) * P],
                                                xhT[:, gp, part_x],
                                                start=(part_w + part_x == 0), stop=(part_w == 1))
                    last.then_inc(f_h, 1)

            def second(n, lp, e):
                pe.wait_ge(f_gelu, E * GT * n + GT * e + GT + 3)
                pe.wait_ge(f_sum, FS0 + E * n + e - 1)
                for s in range(GT):
                    for c in range(GT):
                        last = nc.tensor.matmul(PS[:, 2 + e % 2, s * P:(s + 1) * P], hT[:, e % 2, c, s * P:(s + 1) * P],
                                                w2_s[:, lp, e * GT + c], start=(c == 0), stop=(c == GT - 1))
                last.then_inc(f_y, 1)

            def begin(first_layer):
                pe.wait_ge(f_lg, LG0)
                bias_of_offset(*first_layer)
                stage_xt(0)
                stage_xh(0)
                stage_route(0, 0, 0)
                stage_ct(0, 0)
                stage_b2(0, 0, 0)
                pe.wait_ge(f_xhTs, 1)

            def step(layer, g, gp, new, more):
                l, pair, lp = layer
                n = l * NG + g
                next_l, _, next_lp = new or layer
                if isinstance(g, int) and g == 0:
                    pe.wait_ge(f_wp, l * E + E)
                pe.wait_ge(f_xhTs, n + 1)
                first(n, lp, gp, 0)
                if new:
                    pe.wait_ge(f_lg, n + 1 + LG0)
                    bias_of_offset(*new)
                if more:
                    stage_xt(n + 1)
                first(n, lp, gp, 1)
                if more:
                    stage_xh(n + 1)
                second(n, lp, 0)
                if more:
                    stage_route(n + 1, next_l, 1 - gp)
                first(n, lp, gp, 2)
                second(n, lp, 1)
                first(n, lp, gp, 3)
                second(n, lp, 2)
                if more:
                    stage_ct(n + 1, 1 - gp)
                second(n, lp, 3)
                if more:
                    stage_b2(n + 1, next_lp, 1 - gp)

            run_layers(pe, begin, step)

        @block.vector
        def _(dve):
            def moments(link, links, src, st, mv, rs, tiles, asked):
                for s in range(tiles):
                    last = nc.vector.bn_stats(st[:, s, :], src(s))
                last.then_inc(link, 1)
                dve.wait_ge(link, links + 1)
                apart(dve)
                for s in range(tiles):
                    last = nc.vector.bn_aggr(mv[:, s, :], st[:, s, :])
                last.then_inc(link, 1)
                dve.wait_ge(link, links + 2)
                nc.vector.tensor_scalar(rs, mv[:, :, 1], EPS, None, ALU.add).then_inc(asked, 1)

            def scaled(src, mv, rs, dst, tiles):
                for s in range(tiles):
                    last = nc.vector.tensor_scalar(dst(s), src(s), mv[:, s, 0:1], rs[:, s:s + 1],
                                                   ALU.subtract, ALU.mult)
                return last

            def normalise(link, links, src, st, mv, rs, dst, tiles, asked, answered, count):
                moments(link, links, src, st, mv, rs, tiles, asked)
                dve.wait_ge(answered, count)
                return scaled(src, mv, rs, dst, tiles)

            dve.wait_ge(weights, 16 * 14)
            dve.wait_ge(a_start, 1)
            nc.vector.tensor_scalar(A_s[:], A_s[:], -1.0, None, ALU.mult).then_inc(prepared, 1)
            nc.vector.tensor_copy(selb[:], sel_t[0:ROWS, :]).then_inc(prepared, 1)
            dve.wait_ge(a_pad, 1)
            with dve.Fori(0, BP) as bp:
                for half in range(2):
                    it = bp * 2 + half
                    for bb in range(2):
                        dve.wait_ge(a_x[bb], 16 * it + 16)
                        moments(a_link, (2 * it + bb) * 2, lambda s: xt[:, bb, s], st_a[:, bb], mv_a[:, bb],
                                rs_a[:, bb], 4, a_var)
                    for bb in range(2):
                        dve.wait_ge(a_rs, 2 * it + bb + 1)
                        scaled(lambda s: xt[:, bb, s], mv_a[:, bb], rs_a[:, bb], lambda s: xn[:, bb, s], 4
                               ).then_inc(a_xn, 1)
                    for bb in range(2):
                        dve.wait_ge(a_xi, 2 * it + bb + 1)
                        for t in range(KC):
                            for h in range(HALVES):
                                tap = chan_s[:, h, t:t + 1]
                                if t == 0:
                                    last = nc.vector.tensor_scalar(conv[:, bb, h], xi[:, bb, h, t:t + TT], tap, None,
                                                                   ALU.mult)
                                else:
                                    last = nc.vector.scalar_tensor_tensor(conv[:, bb, h], xi[:, bb, h, t:t + TT], tap,
                                                                          conv[:, bb, h], ALU.mult, ALU.add)
                            if t < KC - 1:
                                last.then_inc(a_tap, 1)
                                dve.wait_ge(a_tap, (2 * it + bb) * (KC - 1) + t + 1)
                            else:
                                last.then_inc(a_conv, 1)
                        dve.wait_ge(a_conv, 2 * (2 * it + bb) + 1)
                        pad = xi[:, bb, :, 0:KC - 1]
                        if half == 0:
                            nc.vector.tensor_copy(pad, xi[:, bb, :, TT:]).then_inc(a_conv, 1)
                        else:
                            nc.vector.memset(pad, 0.0).then_inc(a_conv, 1)
                    for bb in range(2):
                        dve.wait_ge(a_xp, 2 * it + bb + 1)
                        nc.vector.tensor_copy(bc_t[:, bb], PS[:, 4 * bb + 1, :]).then_inc(a_bc, 1)
                    for bb in range(2):
                        dve.wait_ge(a_mag, 4 * it + 1 + bb)
                        for h in range(HALVES):
                            last = nc.vector.tensor_scalar(rl[:, bb, h], PS[:, 4 * bb + 2 + h, :],
                                                           chan_s[:, h, KC + 1:KC + 2], 0.0, ALU.add, ALU.max)
                        last.then_inc(a_rl, 1)
                    for bb in range(2):
                        dve.wait_ge(a_mag, 4 * it + 3 + bb)
                        nc.vector.tensor_scalar(one_p[:, bb], mag[:, bb], 1.0, None, ALU.add).then_inc(a_onep, 1)
                    for bb in range(2):
                        dve.wait_ge(a_onep, 2 * it + bb + 1)
                        nc.vector.scalar_tensor_tensor(slip[:, bb], one_p[:, bb], 1.0, mag[:, bb], ALU.subtract,
                                                       ALU.subtract).then_inc(a_slip, 1)
                    for bb in range(2):
                        dve.wait_ge(a_ln, 2 * it + bb + 1)
                        dve.wait_ge(a_slip, 2 * it + bb + 1)
                        nc.vector.tensor_tensor(lg[:, bb], lg[:, bb], slip[:, bb], ALU.subtract).then_inc(a_exact, 1)
                    for bb in range(2):
                        dve.wait_ge(a_exact, 2 * it + bb + 1)
                        dve.wait_ge(a_rl, 2 * it + bb + 1)
                        nc.vector.tensor_tensor(dd[:, bb, 0], lg[:, bb], rl[:, bb], ALU.add).then_inc(a_delta, 1)
                    for bb in range(2):
                        dve.wait_ge(a_delta, 2 * it + bb + 1)
                        nc.vector.tensor_tensor(dd[:, bb, 1], dd[:, bb, 0], u_s[:, bb], ALU.mult).then_inc(a_du, 1)
            dve.wait_ge(a_du, 2 * NIT)
            dve.sem_inc(a_end, 1)
            dve.wait_ge(a_p3, 2 * NIT + 2)
            dve.wait_ge(a_end, 4)

            def gate(m):
                dve.wait_ge(post_in, 96 * m + 96)
                dve.wait_ge(post_t, m + 2)
                tok = lambda v: v.rearrange("p b (s t) -> p s t b", s=TS)
                flat = lambda v: v.rearrange("p (s t b) -> p s t b", s=TS, b=2)
                for h in range(HALVES):
                    last = nc.vector.scalar_tensor_tensor(flat(G[:, h]), tok(usz[:, 0, h]),
                                                          chan_s[:, h, KC + 2:KC + 3],
                                                          flat(PS[:, 6, h * TS * P:(h + 1) * TS * P]),
                                                          ALU.mult, ALU.add)
                last.then_inc(g_link, 1)
                dve.wait_ge(g_link, m + 1)
                for h in range(HALVES):
                    last = nc.vector.tensor_tensor(flat(G[:, h]), flat(G[:, h]), tok(usz[:, 1, h]), ALU.mult)
                last.then_inc(g_done, 1)


            def chunk_stats(m):
                dve.wait_ge(out_ready, m + 1)
                nc.vector.scalar_tensor_tensor(xsum, xres, 2.0,
                                               PS[:, 7, 0:TS * H].rearrange("p (s h) -> p s h", h=H),
                                               ALU.mult, ALU.add).then_inc(p_link, 1)
                dve.wait_ge(p_link, m * P_LINKS + 1)
                moments(p_link, m * P_LINKS + 1, lambda s: xsum[:, s], st_m, mv_m, rs_m, TS, p_var)

            def chunk_norm(m):
                dve.wait_ge(x1_out, 16 * m + X0)
                dve.wait_ge(p_rs, m + 1)
                scaled(lambda s: xsum[:, s], mv_m, rs_m, lambda s: x1c[:, s], TS).then_inc(post_done, 1)

            def emit(m, kk, before, post):
                blk = m * NBLK + kk
                dve.wait_ge(bc_in, 32 * (m + 1))
                Bc = bc[:, bass.ds(m % 2 * 2 * TC, TC)].unsqueeze(1).broadcast_to([P, CB, TC])

                def times_b(q, r):
                    if before or q > 1:
                        dve.wait_ge(scan_done, blk * NQ + q - 1)
                    dve.wait_ge(du_ready, blk * NP + 2 * q + r + 1 + DU0)
                    nc.vector.tensor_tensor(seg(dB[:, q % 2])[:, r * CB:(r + 1) * CB, 1:],
                                            PS[:, 2 + r, :].rearrange("p (c t) -> p c t", c=CB), Bc,
                                            ALU.mult).then_inc(mult_done, 1)

                times_b(0, 0)
                for q in range(NQ):
                    times_b(q, 1)
                    if q < NQ - 1:
                        times_b(q + 1, 0)
                    dve.wait_ge(mult_done, blk * NP + 2 * q + 2)
                    dve.wait_ge(exp_done, blk * NP + 2 * q + 2)
                    dve.wait_ge(slot_ready, blk * NQ + q + 1)
                    if q == 0 and kk == 1 and isinstance(m, int):
                        dve.wait_ge(a_rows, NIT * 16 * ROW_STORES + 16)
                    if q == 0:
                        dve.wait_ge(y_done, blk - 1 + Y0)
                        dve.wait_ge(carried, blk - 1 + CARRY0)
                    nc.vector.tensor_tensor_scan(hb[:, kk, q * QD * SEG:(q + 1) * QD * SEG], dA[:, q % 2],
                                                 dB[:, q % 2], 0.0, ALU.mult, ALU.add).then_inc(scan_done, 1)
                    if post and q == Q_GATE:
                        gate(m - 1)
                    if post and q == Q_STATS:
                        chunk_stats(m - 1)
                    if post and q == Q_STATS + 1:
                        chunk_norm(m - 1)

            def tail(m):
                gate(m)
                chunk_stats(m)
                chunk_norm(m)

            run_blocks(dve, emit, tail)
            dve.wait_ge(carried, NCH * NBLK + CARRY0)

            dve.wait_ge(post_done, NCH + POST0)
            dve.wait_ge(f_w[0], F_LOADS)
            nc.vector.memset(order, 0.0).then_inc(f_sum, FS0)
            dve.wait_ge(f_sum, FS0)
            dve.wait_ge(x_in, 32)

            F_LINKS = 12

            def at(v, g, s):
                return v[:, bass.ds(g * GT + s, 1), :].rearrange("p a h -> p (a h)")

            def stage_norm(n, g):
                dve.wait_ge(f_sum, E * n + E)
                dve.wait_ge(f_xhT, n + XH0)
                nc.vector.tensor_copy(xg, X[:, bass.ds(g * GT, GT), :]).then_inc(f_xg, 1)
                normalise(f_link, n * F_LINKS, lambda s: at(X, g, s), st_f, mv_f, rs_f, lambda s: xhs[:, s], GT,
                          f_var, f_rs, n + 1).then_inc(f_xn, 1)

            def stage_xt(n, gp):
                dve.wait_ge(f_xT, n + 1)
                nc.vector.tensor_copy(xTs[:, gp], PS[:, 4, :]).then_inc(f_xTs, 1)

            def each(v):
                return v.unsqueeze(2).broadcast_to([P, GT, E])

            def stage_scores(n, l):
                dve.wait_ge(f_lm, n + 1)
                nc.vector.tensor_tensor(lgt, PS[:, 4, 0:GT * E].rearrange("p (s e) -> p s e", e=E),
                                        rb_s[:, bass.ds(l * E, E)].unsqueeze(1).broadcast_to([P, GT, E]),
                                        ALU.add).then_inc(f_link, 1)
                dve.wait_ge(f_link, n * F_LINKS + 3)
                nc.vector.reduce_max(mx, lgt, AX.X).then_inc(f_link, 1)
                dve.wait_ge(f_link, n * F_LINKS + 4)
                nc.vector.tensor_tensor(lgt, lgt, each(mx), ALU.subtract).then_inc(f_lg, 1)

            def stage_router(n, gp):
                dve.wait_ge(f_rt, n + 1)
                nc.vector.reduce_sum(sm, ex, AX.X).then_inc(f_link, 1)
                dve.wait_ge(f_link, n * F_LINKS + 5)
                nc.vector.reciprocal(sm, sm).then_inc(f_link, 1)
                dve.wait_ge(f_link, n * F_LINKS + 6)
                nc.vector.tensor_tensor(pr, ex, each(sm), ALU.mult).then_inc(f_link, 1)
                dve.wait_ge(f_link, n * F_LINKS + 7)
                for j in range(E):
                    pj = pr[:, :, j:j + 1]
                    if j > 0:
                        last = nc.vector.tensor_tensor(order[:, :, j, 0:j], pj.broadcast_to([P, GT, j]),
                                                       pr[:, :, 0:j], ALU.is_gt)
                    if j < E - 1:
                        last = nc.vector.tensor_tensor(order[:, :, j, j + 1:], pj.broadcast_to([P, GT, E - 1 - j]),
                                                       pr[:, :, j + 1:], ALU.is_ge)
                last.then_inc(f_link, 1)
                dve.wait_ge(f_link, n * F_LINKS + 8)
                nc.vector.reduce_sum(rank, order.rearrange("p s j e -> p s e j"), AX.X).then_inc(f_link, 1)
                dve.wait_ge(f_link, n * F_LINKS + 9)
                nc.vector.scalar_tensor_tensor(selp, rank, 2.0, pr, ALU.is_lt, ALU.mult).then_inc(f_link, 1)
                dve.wait_ge(f_link, n * F_LINKS + 10)
                nc.vector.reduce_sum(sm, selp, AX.X).then_inc(f_link, 1)
                dve.wait_ge(f_link, n * F_LINKS + 11)
                nc.vector.reciprocal(sm, sm).then_inc(f_link, 1)
                dve.wait_ge(f_link, n * F_LINKS + 12)
                cw = comb[:, gp].rearrange("p (s e) -> p s e", e=E)
                nc.vector.tensor_tensor(cw, selp, each(sm), ALU.mult).then_inc(f_cw, 1)
                dve.wait_ge(f_cw, n + 1)
                nc.vector.reduce_sum(csum[:, gp], cw, AX.X).then_inc(f_cs, 1)

            def stage_cts(n, gp):
                dve.wait_ge(f_ct, n + 1)
                nc.vector.tensor_copy(combT[0:E, gp], PS[0:E, 5, :]).then_inc(f_cts, 1)

            def start_sum(n, g, gp):
                dve.wait_ge(f_yb, n + 1)
                dve.wait_ge(f_cs, n + 1)
                for s in range(GT):
                    last = nc.vector.scalar_tensor_tensor(at(X, g, s), at(X, g, s), csum[:, gp, s:s + 1],
                                                          PS[:, 7, s * P:(s + 1) * P], ALU.mult, ALU.add)
                last.then_inc(f_x0, 1)

            def add_expert(n, g, gp, e):
                dve.wait_ge(f_y, FY0 + E * n + e + 1)
                dve.wait_ge(f_x0, n + 1)
                dve.wait_ge(f_sum, FS0 + E * n + e)
                for s in range(GT):
                    last = nc.vector.scalar_tensor_tensor(at(X, g, s), PS[:, 2 + e % 2, s * P:(s + 1) * P],
                                                          comb[:, gp, s * E + e:s * E + e + 1], at(X, g, s),
                                                          ALU.mult, ALU.add)
                last.then_inc(f_sum, 1)

            def split_xh(n, gp):
                dve.wait_ge(f_xhT, n + 1 + XH0)
                nc.vector.tensor_copy(xhT[:, gp, 0], PS[:, 5, :]).then_inc(f_xhu, 1)
                dve.wait_ge(f_xhu, n + 1)
                nc.vector.tensor_tensor(xhT[:, gp, 1], PS[:, 5, :], xhT[:, gp, 0].bitcast(fp32), ALU.subtract).then_inc(f_xhTs, 1)

            def split_w1(l, lp):
                for e in range(E):
                    dve.wait_ge(f_g, E * l + e + 1)
                    nc.vector.tensor_copy(w1p[:, lp, 0, e], w1g[:, lp, e]).then_inc(f_upper, 1)
                for e in range(E):
                    dve.wait_ge(f_upper, E * l + e + 1)
                    nc.vector.tensor_tensor(w1p[:, lp, 1, e], w1g[:, lp, e], w1p[:, lp, 0, e].bitcast(fp32), ALU.subtract
                                            ).then_inc(f_wp, 1)

            def add_bias(l, lp):
                dve.wait_ge(f_bp, l + 1)
                nc.vector.tensor_tensor(bias1[:, lp], PS[:, 4, 0:E * GT], b1_s[:, bass.ds(l * E * GT, E * GT)],
                                        ALU.add).then_inc(f_bias, 1)

            def begin(first_layer):
                add_bias(0, 0)
                stage_norm(0, 0)
                stage_xt(0, 0)
                split_xh(0, 0)
                stage_scores(0, 0)
                stage_router(0, 0)
                stage_cts(0, 0)
                split_w1(0, 0)

            def step(layer, g, gp, new, more):
                l, pair, lp = layer
                n = l * NG + g
                next_l, _, next_lp = new or layer
                if new:
                    add_bias(next_l, next_lp)
                if more:
                    stage_norm(n + 1, 0 if new else g + 1)
                start_sum(n, g, gp)
                if more:
                    stage_xt(n + 1, 1 - gp)
                add_expert(n, g, gp, 0)
                if more:
                    split_xh(n + 1, 1 - gp)
                    stage_scores(n + 1, next_l)
                add_expert(n, g, gp, 1)
                if more:
                    stage_router(n + 1, 1 - gp)
                add_expert(n, g, gp, 2)
                if more:
                    stage_cts(n + 1, 1 - gp)
                if new:
                    split_w1(next_l, next_lp)
                add_expert(n, g, gp, 3)

            run_layers(dve, begin, step)

            O_LINKS = 3
            with dve.Fori(0, NG // 2) as g2:
                for gp in range(2):
                    g = g2 * 2 + gp
                    dve.wait_ge(f_sum, FS0 + NG * NL * E)
                    dve.wait_ge(f_fin, g + FIN0)
                    tiles = lambda v: v[:, bass.ds(g * GT, GT), :]
                    nc.vector.tensor_tensor(xhs, tiles(X), tiles(X1), ALU.add).then_inc(f_fl, 1)
                    dve.wait_ge(f_fl, g * O_LINKS + 1)
                    dve.wait_ge(f_out[gp], 64 * g2 + 64)
                    normalise(f_fl, g * O_LINKS + 1, lambda s: xhs[:, s], st_f, mv_f, rs_f, lambda s: xo[:, gp, s], GT,
                              o_var, o_rs, g + 1).then_inc(f_fin, 1)



_INS = ["x", "vecs", "chan", "a_log", "ident", "sel", "w_in", "w_xproj", "w_dt", "w_out",
        "router_w", "router_b", "ln_g", "ln_b", "w1", "b1", "w2", "b2"]


def kernel(L0_attn_x, L0_attn_ln_w, L0_attn_ln_b, L0_attn_W_in, L0_attn_conv_w, L0_attn_conv_b, L0_attn_W_xproj,
           L0_attn_W_dt, L0_attn_b_dt, L0_attn_A_log, L0_attn_D, L0_attn_W_out, L0_ffn_router_w, L0_ffn_router_b,
           L0_ffn_ln_g, L0_ffn_ln_b, L0_ffn_w1, L0_ffn_b1, L0_ffn_w2, L0_ffn_b2):
    import concourse.bacc as bacc
    from concourse.bass_utils import run_bass_kernel_spmd

    f = lambda v: np.asarray(v)
    halves = lambda v: f(v).reshape(HALVES, P).T[:, :, None]
    sel = np.zeros((PARTS, 2, RI, RI, 2, N), np.float32)
    for b in range(2):
        for i in range(RI):
            sel[:, b, i, i, b, :] = 1.0
    data = {
        "x": f(L0_attn_x),
        "vecs": np.stack([f(L0_attn_ln_w), f(L0_attn_ln_b)], 1),
        "chan": np.concatenate([f(L0_attn_conv_w).reshape(HALVES, P, KC).transpose(1, 0, 2), halves(L0_attn_conv_b),
                                halves(L0_attn_b_dt), halves(L0_attn_D)], 2),
        "a_log": np.concatenate([f(L0_attn_A_log).T] * 2, 0),
        "ident": np.eye(P, dtype=np.float32),
        "sel": sel.reshape(ROWS, RI * P),
        "w_in": f(L0_attn_W_in), "w_xproj": f(L0_attn_W_xproj), "w_dt": f(L0_attn_W_dt), "w_out": f(L0_attn_W_out),
        "router_w": f(L0_ffn_router_w).transpose(1, 0, 2).reshape(H, NL * E),
        "router_b": np.concatenate([f(L0_ffn_router_b).reshape(1, NL * E)] * P, 0),
        "ln_g": f(L0_ffn_ln_g).reshape(NL * E, H).T,
        "ln_b": f(L0_ffn_ln_b).reshape(NL * E, H).T,
        "w1": f(L0_ffn_w1),
        "b1": f(L0_ffn_b1).reshape(NL * E * GT, P).T,
        "w2": f(L0_ffn_w2),
        "b2": f(L0_ffn_b2),
    }
    nc = bacc.Bacc("TRN2", target_bir_lowering=False, num_devices=1)
    arrays, args = {}, []
    for name in _INS:
        a = np.ascontiguousarray(data[name])
        arrays[f"in_{name}"] = a
        args.append(nc.dram_tensor(f"in_{name}", a.shape, mybir.dt.from_np(a.dtype), kind="ExternalInput").ap())
    out = nc.dram_tensor("out_dram", (B, L, H), mybir.dt.float32, kind="ExternalOutput").ap()
    build(nc, *args, out)
    r = run_bass_kernel_spmd(nc, [arrays], core_ids=[0])
    return r.results[0]["out_dram"]
```

```python
from contextlib import ExitStack

import numpy as np

import concourse.bass as bass
from concourse import mybir

B, L, H = 4, 1024, 128
DI, N, R, KC = 256, 64, 8, 4
NL, E, F = 4, 4, 512
P = 128
HALVES = DI // P
BP = B // 2
TC = 128
NCH = BP * (L // TC)
DB = 128
NBLK = DI // DB
CB = 512 // TC
QD = 2 * CB
NQ = DB // QD
NP = DB // CB
PARTS = 3
RI = 16
ROWS = PARTS * 2 * RI
NRT = NP // RI
CPT = 4
SEG = TC + 1
TS = TC // 64
NT = NCH * TS
TT = 512
NIT = BP * (L // TT)
EPS = 1e-5
IBLK = 544
GT = 4
NG = NT // GT
SLOTS = NCH // BP + 1


def build(nc, x, vecs, chan, a_log, ident, sel, w_in, w_xproj, w_dt, w_out,
          router_w, router_b, ln_g, ln_b, w1, b1, w2, b2, out):
    fp32 = mybir.dt.float32
    bf16 = mybir.dt.bfloat16
    fp32r = mybir.dt.float32r
    ALU = mybir.AluOpType
    ACT = mybir.ActivationFunctionType
    AX = mybir.AxisListType

    rows_d = nc.dram_tensor("rows_d", (NIT, 2, DI // 64, ROWS, CB, TT), bf16).ap()
    bc_d = nc.dram_tensor("bc_d", (NIT, 2, P, TT), fp32).ap()
    x1_d = nc.dram_tensor("x1_d", (NCH, P, TS, H), fp32).ap()
    u_d = nc.dram_tensor("u_d", (NIT, 2, DI, TT), fp32).ap()
    sz_d = nc.dram_tensor("sz_d", (NIT, 2, DI, TT), fp32).ap()

    ctx = ExitStack()
    with ctx:
        def sb(name, shape, dt=fp32):
            return ctx.enter_context(nc.sbuf_tensor(name, shape, dt))

        def sem(name):
            return ctx.enter_context(nc.semaphore(name))

        PS = ctx.enter_context(nc.psum_tensor("PS", [P, 8, 512], fp32))

        ident_s = sb("ident_s", [P, P])
        selb = sb("selb", [ROWS, RI * P], bf16)
        vecs_s = sb("vecs_s", [P, 2])
        chan_s = sb("chan_s", [P, HALVES, KC + 3])
        A_s = sb("A_s", [P, DI])
        wout_s = sb("wout_s", [P, HALVES, H])
        rb_s = sb("rb_s", [P, NL * E])
        g_s = sb("g_s", [P, NL * E])
        lb_s = sb("lb_s", [P, NL * E])
        b1_s = sb("b1_s", [P, NL * E * GT])

        carry = sb("carry", [P, SLOTS, DI])

        neg_half = sb("neg_half", [P, 4])
        euler = sb("euler", [P, 1])

        ARENA = 36200
        arena = sb("arena", [P, ARENA])
        BEHIND = 11100
        with nc.sbuf_tensor("behind", [P, BEHIND], fp32) as behind:
            pass
        parts_w1 = sb("parts_w1", [P, 2 * 2 * E * F], fp32r)
        parts_xh = sb("parts_xh", [P, 2 * 2 * GT * P], fp32r)

        at_, space, limit = [0], [arena], [ARENA]

        def shaped(v, shape):
            if len(shape) == 2:
                v = v.rearrange("p (a b) -> p a b", b=shape[1])
            elif len(shape) == 3:
                v = v.rearrange("p (a b c) -> p a b c", b=shape[1], c=shape[2])
            elif len(shape) == 4:
                v = v.rearrange("p (a b c d) -> p a b c d", b=shape[1], c=shape[2], d=shape[3])
            return v

        def carve(n):
            at_[0] += n
            assert at_[0] <= limit[0], at_[0]
            return space[0][:, at_[0] - n:at_[0]]

        def take(*shape):
            return shaped(carve(int(np.prod(shape))), shape)

        def take_bf16(*shape):
            return shaped(carve(int(np.prod(shape)) // 2).bitcast(bf16), shape)

        at_[0] = 0
        xt = take(2, 4, H)
        xn = take(2, 4, H)
        xnT = take(2, TT)
        xi = take(2, HALVES, KC - 1 + TT)
        conv = take(2, HALVES, TT)
        u_s = take(2, HALVES, TT)
        sz_s = take(2, HALVES, TT)
        dtr_s = take(2, TT)
        rest = take(2, 2, HALVES, TT)
        mag, one_p = rest[:, 0], rest[:, 1]
        slip = take(2, HALVES, TT)
        assert at_[0] >= DB * SEG
        part = [[take_bf16(2, HALVES, TT) for _ in range(PARTS)] for _ in range(2)]
        assert at_[0] <= 2 * DB * SEG
        lg = take(2, HALVES, TT)
        rl = take(2, HALVES, TT)
        dd = take(2, 2, HALVES, TT)
        bc_t = take(2, TT)
        win_s = take(4 * P)
        wx_s = take(HALVES, R + 2 * N)
        wdt_s = take(DI)
        st_a = take(2, 4, 6)
        mv_a = take(2, 4, 2)
        rs_a = take(2, 4)

        at_[0] = 0
        hb = take(2, DB * SEG)
        usz = take(2, HALVES, 2, TC)
        xres = take(TS, H)
        G = take(HALVES, TS * P)
        ysb = take(TS, DI)
        xsum = take(TS, H)
        X1C_AT = at_[0]
        x1c = take(TS, H)
        st_m = take(TS, 6)
        mv_m = take(TS, 2)
        rs_m = take(TS)
        at_[0] = 0
        space[0], limit[0] = behind, BEHIND
        dA = take(2, QD * SEG)
        dB = take(2, QD * SEG)
        rows = take_bf16(2, 2 * NRT, 512)
        bc = take(2 * 2 * TC)
        sel_t = behind[:, at_[0]:at_[0] + RI * P]
        cd = take(TS * 4, IBLK)

        space[0], limit[0] = arena, ARENA
        at_[0] = 0
        w1_s = take(2, E, F)
        w1g = take(E, F)
        w1p = parts_w1[:].rearrange("p (l w e f) -> p l w e f", l=2, w=2, e=E)
        xhT = parts_xh[:].rearrange("p (g w t) -> p g w t", g=2, w=2)
        w2_s = take(2, E * GT, H)
        bias1 = take(2, E * GT)
        rw_s = take(NL, E, H)
        X = take(NT, H)
        assert at_[0] <= DB * SEG
        X1 = take(NT, H)
        scored = take(GT, E, H)
        b2_s = take(NL, E, H)
        weighted = take(GT, E, H)
        bias2 = take(GT, H)
        xhs = take(GT, P)
        hT = take(2, GT, 512)
        lgt = take(GT, E)
        mx = take(GT)
        ex = take(GT, E)
        sm = take(GT)
        pr = take(GT, E)
        rank = take(GT, E)
        order = take(GT, E, E)
        selp = take(GT, E)
        comb = take(2, GT * E)
        csum = take(2, GT)
        st_f = take(GT, 6)
        mv_f = take(GT, 2)
        rs_f = take(GT)
        xo = take(2, GT, H)
        xsum_o = take(GT, H)
        st_o = take(GT, 6)
        mv_o = take(GT, 2)
        rs_o = take(GT)
        assert at_[0] <= X1C_AT

        passed = sem("passed")
        a_var = sem("a_var")
        a_rs = sem("a_rs")
        p_var = sem("p_var")
        p_rs = sem("p_rs")
        f_var = sem("f_var")
        f_rs = sem("f_rs")
        o_var = sem("o_var")
        o_rs = sem("o_rs")
        weights = sem("weights")
        a_start = sem("a_start")
        zeroed = sem("zeroed")
        prepared = sem("prepared")
        a_x = [sem(f"a_x{i}") for i in range(2)]
        a_xn = sem("a_xn")
        a_tp = sem("a_tp")
        a_xnT = sem("a_xnT")
        a_xip = sem("a_xip")
        a_zp = sem("a_zp")
        a_dtp = sem("a_dtp")
        a_xi = sem("a_xi")
        a_pad = sem("a_pad")
        a_conv = sem("a_conv")
        a_u = sem("a_u")
        a_sz = sem("a_sz")
        a_xp = sem("a_xp")
        a_bc = sem("a_bc")
        a_dtr = sem("a_dtr")
        a_v = sem("a_v")
        a_mag = sem("a_mag")
        a_onep = sem("a_onep")
        a_slip = sem("a_slip")
        a_ln = sem("a_ln")
        a_p1 = sem("a_p1")
        a_rest = sem("a_rest")
        a_p2 = sem("a_p2")
        a_p3 = sem("a_p3")
        a_bcs = sem("a_bcs")
        a_delta = sem("a_delta")
        a_du = sem("a_du")
        a_stored = sem("a_stored")
        a_rows = sem("a_rows")
        a_link = sem("a_link")
        a_tap = sem("a_tap")
        a_rl = sem("a_rl")
        a_exact = sem("a_exact")
        a_end = sem("a_end")
        arg_ready = sem("arg_ready")
        du_ready = sem("du_ready")
        exp_done = sem("exp_done")
        mult_done = sem("mult_done")
        scan_done = sem("scan_done")
        slot_ready = sem("slot_ready")
        carried = sem("carried")
        y_done = sem("y_done")
        evacuated = sem("evacuated")
        c_spread = sem("c_spread")
        bc_in = sem("bc_in")
        x1_out = sem("x1_out")
        x_in = sem("x_in")
        post_in = sem("post_in")
        post_t = sem("post_t")
        skipped = sem("skipped")
        g_done = sem("g_done")
        out_ready = sem("out_ready")
        p_link = sem("p_link")
        post_done = sem("post_done")
        f_g = sem("f_g")
        f_bp = sem("f_bp")
        f_bias = sem("f_bias")
        f_xhT = sem("f_xhT")
        f_xhTs = sem("f_xhTs")
        f_lg = sem("f_lg")
        f_link = sem("f_link")
        f_rt = sem("f_rt")
        f_h = sem("f_h")
        f_gelu = sem("f_gelu")
        f_y = sem("f_y")
        f_yb = sem("f_yb")
        f_scored = sem("f_scored")
        rw_in = sem("rw_in")
        b2_in = sem("b2_in")
        f_weighted = sem("f_weighted")
        f_last = sem("f_last")
        f_xhu = sem("f_xhu")
        f_upper = sem("f_upper")
        f_wp = sem("f_wp")
        f_xn = sem("f_xn")
        f_lm = sem("f_lm")
        f_cw = sem("f_cw")
        f_cs = sem("f_cs")
        f_x0 = sem("f_x0")
        f_sum = sem("f_sum")
        f_fin = sem("f_fin")
        f_fl = sem("f_fl")
        rows_in = [sem(f"rows_in{i}") for i in range(2)]
        f_w = [sem(f"f_w{i}") for i in range(2)]
        f_out = [sem(f"f_out{i}") for i in range(2)]

        CARRY0, Y0, EV0, POST0, FIN0, DU0, X0, LG0, XH0 = NBLK, 2, 2, 1, 1, 1, 16, 1, 1
        A_STORES = 2 * (2 + 1)
        ROW_STORES = 2 * PARTS * 2
        F_LOADS = 16 * (E + 1)
        FS0, FY0 = NG * E, 2 * NG * E
        P_LINKS = 3
        HIDDEN = (0, 1, 6)
        LEAD = 0
        P_SUM, SUM_PARTS, P_EVACUATE = 4, 24, 30
        P_TURN, Q_GATE, P_PROJECT, Q_STATS, P_STORE = 0, 2, 12, 7, 24

        block = ctx.enter_context(nc.Block())

        def run_layers(eng, begin, step):
            def layer(at_layer, following):
                step(at_layer, 0, 0, None, True)
                with eng.Fori(0, NG // 2 - 1) as g2:
                    for gp in range(2):
                        step(at_layer, g2 * 2 + gp + 1, 1 - gp, None, True)
                step(at_layer, NG - 1, 1, following, following is not None)

            begin((0, 0, 0))
            layer((0, 0, 0), (1, 0, 1))
            with eng.Fori(1, NL // 2) as l2:
                layer((l2 * 2 - 1, l2 - 1, 1), (l2 * 2, l2, 0))
                layer((l2 * 2, l2, 0), (l2 * 2 + 1, l2, 1))
            layer((NL - 1, NL // 2 - 1, 1), None)

        def apart(eng):
            eng.sem_inc(passed, 1)

        def tokens(v, m, s):
            pair, c = m // (NCH // BP), m % (NCH // BP)
            return v[bass.ds(pair * 2, 2), bass.ds(c * TC + s * 64, 64), :].rearrange("b t h -> t b h")

        def load_bc(eng, m):
            for b in range(2):
                eng.dma_start(bc[N * b:N * b + N, bass.ds(m % 2 * 2 * TC, 2 * TC)].rearrange("n (i t) -> n i t", t=TC),
                              bc_d[m // CPT, b, :, bass.ds(m % CPT * TC, TC)].rearrange("(i n) t -> n i t", n=N)
                              ).then_inc(bc_in, 16)

        def load_rows(eng, m, kk):
            for v in range(2):
                for g in range(NRT):
                    eng.dma_start(rows[0:ROWS, kk, v * NRT + g, :].rearrange("r (j t) -> r j t", t=TC),
                                  rows_d[m // CPT, v, kk * NRT + g, :, :, bass.ds(m % CPT * TC, TC)]
                                  ).then_inc(rows_in[kk], 16)

        def by_token(v):
            return v.rearrange("p b (s t) -> p s t b", s=TS)

        def by_step(v):
            return v.rearrange("p (s t b) -> p s t b", s=TS, b=2)

        def seg(v):
            return v.rearrange("p (c s) -> p c s", s=SEG)

        def run_blocks(eng, emit, tail):
            emit(0, 0, 0, 0)
            for kk in range(1, NBLK):
                emit(0, kk, 1, 0)
            with eng.Fori(1, NCH) as m:
                for kk in range(NBLK):
                    emit(m, kk, 1, int(kk == 1))
            tail(NCH - 1)

        @block.sync
        def _(sp):
            def load_x(pair, half, bb):
                sp.dma_start(xt[:, bb], x[bass.ds(pair * 2 + bb, 1), half * TT:(half + 1) * TT, :]
                             .rearrange("b (s p) h -> p (b s) h", p=P)).then_inc(a_x[bb], 16)

            for bb in range(2):
                load_x(0, 0, bb)
            for dst, src in ((ident_s[:], ident), (sel_t[0:ROWS, :], sel), (vecs_s[:], vecs),
                             (chan_s[:], chan), (A_s[:], a_log),
                             (win_s, w_in), (wx_s, w_xproj.rearrange("(h p) n -> p h n", p=P)),
                             (wdt_s[0:R, :], w_dt), (wout_s[:], w_out.rearrange("(h p) n -> p h n", p=P)),
                             (rb_s[:], router_b), (g_s[:], ln_g), (lb_s[:], ln_b),
                             (b1_s[:], b1)):
                sp.dma_start(dst, src).then_inc(weights, 16)

            with sp.Fori(0, BP) as bp:
                for half in range(2):
                    it = bp * 2 + half
                    m0 = bp * 8 + half * CPT
                    for bb in range(2):
                        sp.wait_ge(a_xn, 2 * it + bb + 1)
                        load_x((bp + half) % BP, 1 - half, bb)
                    for bb in range(2):
                        sp.wait_ge(a_sz, 2 * it + bb + 1)
                        sp.wait_ge(a_u, 2 * it + bb + 1)
                        apart(sp)
                        for dram, s in ((u_d, u_s), (sz_d, sz_s)):
                            sp.dma_start(dram[it, bb].rearrange("(h p) t -> p h t", p=P), s[:, bb]
                                         ).then_inc(a_stored, 16)
                    for bb in range(2):
                        sp.wait_ge(a_bc, 2 * it + bb + 1)
                        apart(sp)
                        sp.dma_start(bc_d[it, bb], bc_t[:, bb]).then_inc(a_stored, 16)
                    for bb in range(2):
                        sp.wait_ge(a_p3, 2 * it + bb + 3)
                        apart(sp)
                        for w in range(PARTS):
                            for gl in range(2):
                                r0 = w * 2 * RI + bb * RI
                                sp.dma_start(
                                    rows_d[it].rearrange("v (gh gl) r j t -> gl r j (v gh) t", gl=2)
                                    [gl, r0:r0 + RI].rearrange("i j q t -> (i j) q t"),
                                    part[bb][w][64 * gl:64 * gl + 64].rearrange("p v h t -> p (v h) t")
                                    ).then_inc(a_rows, 16)
            for bb in range(2):
                sp.wait_ge(a_x[bb], 16 * NIT + 16)
            sp.wait_ge(a_stored, NIT * 16 * A_STORES + 16)
            sp.sem_inc(a_end, 1)
            sp.wait_ge(a_end, 4)
            sp.wait_ge(a_rows, NIT * 16 * ROW_STORES + 16)

            def emit(m, kk, before, post):
                blk = m * NBLK + kk
                if before:
                    sp.wait_ge(du_ready, (blk - 1) * NP + DU0)
                    apart(sp)
                    if kk == 0:
                        sp.wait_ge(bc_in, 32 * m)
                        apart(sp)
                        load_bc(sp, m)
                    load_rows(sp, m, kk)
                if kk == 1:
                    sp.wait_ge(post_done, m + POST0)
                    apart(sp)
                    for i, dram in enumerate((u_d, sz_d)):
                        for h in range(HALVES):
                            sp.dma_start(usz[:, i, h, :, :], dram[m // CPT, :, h * P:(h + 1) * P,
                                                                  bass.ds(m % CPT * TC, TC)]
                                         .rearrange("b p t -> p b t")).then_inc(post_in, 16)
                    for s in range(TS):
                        sp.dma_start(xres[:, s, :], tokens(x, m, s)).then_inc(post_in, 16)

            run_blocks(sp, emit, lambda m: None)

            sp.wait_ge(y_done, NCH * NBLK - 1 + Y0)
            sp.wait_ge(carried, NCH * NBLK - 1 + CARRY0)
            sp.wait_ge(x1_out, 16 * (NCH - 1) + X0)
            chunks = lambda v, lo, hi: v.rearrange("p (m s) h -> p m (s h)", s=TS)[:, lo:hi]
            stored = lambda lo, hi: x1_d[lo:hi].rearrange("m p s h -> p m (s h)")
            sp.dma_start(chunks(X, 0, NCH - 1), stored(0, NCH - 1)).then_inc(x_in, 16)
            sp.dma_start(rw_s, router_w.rearrange("p (l e h) -> p l e h", l=NL, e=E)).then_inc(rw_in, 16)
            with sp.Fori(0, NL // 2) as l2:
                for lp in range(2):
                    l = l2 * 2 + lp
                    sp.wait_ge(f_y, NG * E * (l + 1))
                    sp.dma_start(w1_s[:, lp],
                                 w1[l].rearrange("e h f -> h e f")).then_inc(f_w[lp], 16)
                    for e in range(E):
                        sp.dma_start(w2_s[:, lp, e * GT:(e + 1) * GT], w2[l, e].rearrange("(c p) h -> p c h", p=P)
                                     ).then_inc(f_w[lp], 16)
            sp.wait_ge(x1_out, 16 * NCH + X0)
            sp.dma_start(chunks(X1, 0, NCH), stored(0, NCH)).then_inc(x_in, 16)
            with sp.Fori(0, NG // 2) as g2:
                for gp in range(2):
                    g = g2 * 2 + gp
                    sp.wait_ge(f_fin, g + 1 + FIN0)
                    apart(sp)
                    for s in range(GT):
                        sp.dma_start(tokens(out, g * (GT // TS) + s // TS, s % TS), xo[:, gp, s, :]
                                     ).then_inc(f_out[gp], 16)
            sp.wait_ge(f_out[0], 8 * NT + 64)
            sp.wait_ge(f_out[1], 8 * NT + 64)

        @block.gpsimd
        def _(pool):
            nc.gpsimd.memset(xi[:, :, :, 0:KC - 1], 0.0).then_inc(a_pad, 1)
            nc.gpsimd.memset(carry[:], 0.0).then_inc(zeroed, 1)
            nc.gpsimd.memset(neg_half[:], -0.5).then_inc(zeroed, 1)
            nc.gpsimd.memset(euler[:], float(np.e)).then_inc(zeroed, 1)
            pool.wait_ge(zeroed, 3)

            def rsqrt(rs, asked, answered, count):
                pool.wait_ge(asked, count)
                nc.gpsimd.tensor_tensor(rs, rs, neg_half[:, 0:rs.shape[-1]], ALU.pow).then_inc(answered, 1)
                pool.wait_ge(answered, count)
                apart(pool)

            pool.sem_inc(a_stored, 16)
            pool.sem_inc(a_rows, 16)
            pool.sem_inc(a_p3, 2)
            pool.sem_inc(a_rl, 2)
            pool.sem_inc(a_tp, 2)
            pool.sem_inc(carried, CARRY0)
            pool.sem_inc(y_done, Y0)
            pool.sem_inc(evacuated, EV0)
            pool.sem_inc(post_done, POST0)
            pool.sem_inc(du_ready, DU0)
            pool.sem_inc(x1_out, X0)
            pool.sem_inc(post_t, 1)
            pool.sem_inc(f_lg, LG0)
            pool.sem_inc(f_x0, 1)
            pool.sem_inc(f_yb, 1)
            pool.sem_inc(f_rt, LG0)
            pool.sem_inc(f_lm, LG0)
            pool.sem_inc(f_xhT, XH0)
            pool.sem_inc(f_y, FY0)
            pool.sem_inc(f_gelu, 3)
            pool.sem_inc(f_fin, FIN0)
            pool.sem_inc(f_out[0], 64)
            pool.sem_inc(f_out[1], 64)
            for bb in range(2):
                rsqrt(rs_a[:, bb], a_var, a_rs, bb + 1)
            nc.gpsimd.memset(dA, 0.0).then_inc(prepared, 1)
            pool.wait_ge(prepared, 3)
            nc.gpsimd.memset(cd, 0.0).then_inc(zeroed, 1)
            pool.wait_ge(zeroed, 4)
            with pool.Fori(0, BP) as bp:
                for half in range(2):
                    it = bp * 2 + half
                    for bb in range(2):
                        rsqrt(rs_a[:, bb], a_var, a_rs, 2 * it + bb + 3)
                    for bb in range(2):
                        pool.wait_ge(a_p2, 2 * it + bb + 1)
                        nc.gpsimd.tensor_tensor(part[bb][2], rest[:, bb], part[bb][1], ALU.subtract).then_inc(a_p3, 1)
            pool.wait_ge(a_p3, 2 * NIT + 2)
            pool.wait_ge(a_end, 4)
            def gate(m):
                pool.wait_ge(skipped, m + 1)
                for h in range(HALVES):
                    last = nc.gpsimd.tensor_tensor(by_step(G[:, h]), by_step(G[:, h]), by_token(usz[:, 1, h]),
                                                   ALU.mult)
                last.then_inc(g_done, 1)

            def emit(m, kk, before, post):
                blk = m * NBLK + kk
                if kk == 1:
                    pool.wait_ge(y_done, blk - 1 + Y0)
                    pool.wait_ge(bc_in, 32 * (m + 1))
                    pool.wait_ge(carried, blk + CARRY0)
                    for b in range(2):
                        dst = cd[64 * b:64 * b + 64].rearrange("p g (i s) -> p g i s", s=34)[:, :, :, b]
                        src = bc[64 * b:64 * b + 64, bass.ds(m % 2 * 2 * TC + TC, TC)].rearrange(
                            "p (g i) -> p g i", i=16)
                        nc.gpsimd.tensor_copy(dst, src).then_inc(c_spread, 1)
                    pool.wait_ge(c_spread, 2 * m + 2)
                pool.wait_ge(carried, blk - NBLK + 1 + CARRY0)
                slot = m % (NCH // BP)
                for q in range(NQ):
                    if before or q > 1:
                        pool.wait_ge(scan_done, blk * NQ + q - 1)
                    nc.gpsimd.tensor_copy(seg(dB[:, q % 2])[:, :, 0],
                                          carry[:, slot, kk * DB + q * QD:kk * DB + (q + 1) * QD]
                                          ).then_inc(slot_ready, 1)
                    if post and q == Q_GATE + 1:
                        gate(m - 1)
                    if post and q == Q_STATS + 2:
                        rsqrt(rs_m, p_var, p_rs, m)
                pool.wait_ge(scan_done, blk * NQ + NQ)
                nc.gpsimd.tensor_copy(carry[:, slot + 1, kk * DB:(kk + 1) * DB],
                                      seg(hb[:, kk])[:, :, TC]).then_inc(carried, 1)

            def prepare(l, pair, lp):
                pool.wait_ge(f_w[lp], F_LOADS * (pair + 1))
                if not isinstance(l, int) or l > 0:
                    pool.wait_ge(f_wp, E * l)
                for e in range(E):
                    nc.gpsimd.tensor_tensor(w1g[:, e], w1_s[:, lp, e],
                                            g_s[:, bass.ds(l * E + e, 1)].broadcast_to([P, F]), ALU.mult
                                            ).then_inc(f_g, 1)

            def tail(m):
                pool.wait_ge(y_done, NCH * NBLK - 1 + Y0)
                prepare(0, 0, 0)
                gate(m)
                rsqrt(rs_m, p_var, p_rs, m + 1)

            run_blocks(pool, emit, tail)

            def stage_exp(n):
                pool.wait_ge(f_lg, n + 1 + LG0)
                nc.gpsimd.tensor_tensor(ex, euler[:].unsqueeze(2).broadcast_to([P, GT, E]), lgt, ALU.pow
                                        ).then_inc(f_rt, 1)

            def stage_scores(n, g, l):
                pool.wait_ge(f_sum, E * n + E)
                pool.wait_ge(f_lm, n + LG0)
                nc.gpsimd.tensor_tensor(scored, X[:, bass.ds(g * GT, GT), :].unsqueeze(2).broadcast_to([P, GT, E, H]),
                                        rw_s[:, bass.ds(l, 1)].broadcast_to([P, GT, E, H]), ALU.mult
                                        ).then_inc(f_scored, 1)

            def stage_bias(n, l, gp):
                pool.wait_ge(f_cw, n + 1)
                pool.wait_ge(f_yb, n + 1)
                nc.gpsimd.tensor_tensor(weighted, b2_s[:, bass.ds(l, 1)].broadcast_to([P, GT, E, H]),
                                        comb[:, gp].rearrange("p (s e) -> p s e", e=E).unsqueeze(3).broadcast_to(
                                            [P, GT, E, H]), ALU.mult).then_inc(f_weighted, 1)

            def begin(first_layer):
                pool.wait_ge(f_last, 1)
                pool.wait_ge(rw_in, 16)
                rsqrt(rs_f, f_var, f_rs, 1)
                stage_scores(0, 0, 0)
                stage_exp(0)
                pool.wait_ge(b2_in, 16)
                stage_bias(0, 0, 0)

            def step(layer, g, gp, new, more):
                n = layer[0] * NG + g
                if more:
                    rsqrt(rs_f, f_var, f_rs, n + 2)
                    stage_scores(n + 1, 0 if new else g + 1, new[0] if new else layer[0])
                if new:
                    prepare(*new)
                if more:
                    stage_exp(n + 1)
                    stage_bias(n + 1, new[0] if new else layer[0], 1 - gp)
                if isinstance(layer[0], int) and layer[0] == NL - 1 and not (isinstance(g, int) and g == 0):
                    rsqrt(rs_o, o_var, o_rs, g)

            run_layers(pool, begin, step)
            rsqrt(rs_o, o_var, o_rs, NG)

        @block.scalar
        def _(act):
            act.wait_ge(weights, 16 * 13)
            nc.scalar.activation(A_s[:], A_s[:], ACT.Exp).then_inc(a_start, 1)
            with act.Fori(0, BP) as bp:
                for half in range(2):
                    it = bp * 2 + half
                    for bb in range(2):
                        act.wait_ge(a_tp, 2 * it + bb + 3)
                        nc.scalar.activation(xnT[:, bb], PS[:, 4 * bb + 3, :], ACT.Identity, bias=vecs_s[:, 1:2],
                                             scale=vecs_s[:, 0:1]).then_inc(a_xnT, 1)
                    for bb in range(2):
                        act.wait_ge(a_xip, 2 * it + bb + 1)
                        nc.scalar.activation(xi[:, bb, :, KC - 1:], PS[:, 4 * bb:4 * bb + 2, :], ACT.Identity
                                             ).then_inc(a_xi, 1)
                    act.wait_ge(a_stored, it * 16 * A_STORES + 16)
                    for bb in range(2):
                        act.wait_ge(a_zp, 2 * it + bb + 1)
                        nc.scalar.activation(sz_s[:, bb], PS[:, 4 * bb + 2:4 * bb + 4, :], ACT.Silu).then_inc(a_sz, 1)
                    for bb in range(2):
                        act.wait_ge(a_conv, 2 * (2 * it + bb) + 1)
                        for h in range(HALVES):
                            last = nc.scalar.activation(u_s[:, bb, h], conv[:, bb, h], ACT.Silu,
                                                        bias=chan_s[:, h, KC:KC + 1])
                        last.then_inc(a_u, 1)
                    for bb in range(2):
                        act.wait_ge(a_dtp, 2 * it + bb + 1)
                        nc.scalar.activation(dtr_s[0:R, bb, :], PS[0:R, 4 * bb, :], ACT.Identity).then_inc(a_dtr, 1)
                    act.wait_ge(a_p3, 2 * it + 2)
                    for bb in range(2):
                        act.wait_ge(a_v, 2 * it + bb + 1)
                        for h in range(HALVES):
                            last = nc.scalar.activation(mag[:, bb, h], PS[:, 4 * bb + 2 + h, :], ACT.Abs,
                                                        bias=chan_s[:, h, KC + 1:KC + 2])
                        last.then_inc(a_mag, 1)
                    for bb in range(2):
                        act.wait_ge(a_mag, 4 * it + 2 + bb)
                        nc.scalar.activation(mag[:, bb], mag[:, bb], ACT.Exp, scale=-1.0).then_inc(a_mag, 1)
                    for bb in range(2):
                        act.wait_ge(a_onep, 2 * it + bb + 1)
                        nc.scalar.activation(lg[:, bb], one_p[:, bb], ACT.Ln).then_inc(a_ln, 1)
                    act.wait_ge(a_rows, it * 16 * ROW_STORES + 16)
                    for bb in range(2):
                        act.wait_ge(a_du, 2 * it + bb + 1)
                        nc.scalar.activation(part[bb][0], dd[:, bb], ACT.Identity).then_inc(a_p1, 1)
                    for bb in range(2):
                        act.wait_ge(a_rest, 2 * it + bb + 1)
                        nc.scalar.activation(part[bb][1], rest[:, bb], ACT.Identity).then_inc(a_p2, 1)
            load_bc(act, 0)
            load_rows(act, 0, 0)
            act.wait_ge(a_ln, 2 * NIT)
            act.sem_inc(a_end, 1)
            act.wait_ge(prepared, 3)

            def evacuate(m, kk):
                act.wait_ge(y_done, m * NBLK + kk + 1 + Y0)
                if kk == 0:
                    act.wait_ge(post_t, m + 1)
                nc.scalar.activation(ysb[:, :, kk * DB:(kk + 1) * DB],
                                     PS[:, 4 + kk, 0:TS * DB].rearrange("p (s d) -> p s d", d=DB),
                                     ACT.Identity).then_inc(evacuated, 1)

            def store_x1(m):
                act.wait_ge(post_done, m + 1 + POST0)
                act.dma_start(x1_d[m], x1c).then_inc(x1_out, 16)

            def emit(m, kk, before, post):
                blk = m * NBLK + kk
                for p in range(NP):
                    q = p // 2
                    if p % 2 == 0 and (before or q > 1):
                        act.wait_ge(scan_done, blk * NQ + q - 1)
                    act.wait_ge(arg_ready, blk * NP + p + 1)
                    for j in range(CB):
                        d = kk * DB + CB * p + j
                        c = (p % 2) * CB + j
                        last = nc.scalar.activation(dA[:, q % 2, c * SEG + 1:(c + 1) * SEG],
                                                    PS[:, p % 2, j * TC:(j + 1) * TC], ACT.Exp,
                                                    scale=A_s[:, d:d + 1])
                    last.then_inc(exp_done, 1)
                    if before and p == P_EVACUATE:
                        evacuate(m if kk else m - 1, 1 - kk)
                    if post and p == P_STORE:
                        store_x1(m - 1)

            def tail(m):
                evacuate(m, NBLK - 1)
                act.wait_ge(carried, NCH * NBLK + CARRY0)
                act.dma_start(b2_s, b2.rearrange("p (l e h) -> p l e h", l=NL, e=E)).then_inc(b2_in, 16)
                store_x1(m)

            run_blocks(act, emit, tail)

            def step(layer, g, gp, new, more):
                l, pair, lp = layer
                n = l * NG + g
                if isinstance(g, int) and g == 0:
                    act.wait_ge(f_bias, l + 1)
                for e in range(E):
                    act.wait_ge(f_y, FY0 + E * n + e - 1)
                    for c in range(GT):
                        act.wait_ge(f_h, E * GT * n + GT * e + c + 1)
                        nc.scalar.activation(hT[:, e % 2, c], PS[:, HIDDEN[(GT * e + c) % 3], :], ACT.Gelu,
                                             bias=bias1[:, lp, e * GT + c:e * GT + c + 1]
                                             ).then_inc(f_gelu, 1)

            run_layers(act, lambda first_layer: None, step)

        @block.tensor
        def _(pe):
            pe.wait_ge(weights, 16 * 13)
            with pe.Fori(0, BP) as bp:
                for half in range(2):
                    it = bp * 2 + half
                    pe.wait_ge(a_rl, 2 * it + 2)
                    for bb in range(2):
                        pe.wait_ge(a_xn, 2 * it + bb + 1)
                        for s in range(4):
                            last = nc.tensor.transpose(PS[:, 4 * bb + 3, s * P:(s + 1) * P], xn[:, bb, s], ident_s[:])
                        last.then_inc(a_tp, 1)
                    for bb in range(2):
                        pe.wait_ge(a_xnT, 2 * it + bb + 1)
                        for c in range(2):
                            last = nc.tensor.matmul(PS[:, 4 * bb + c, :], win_s[:, c * P:(c + 1) * P], xnT[:, bb],
                                                    start=True, stop=True)
                        last.then_inc(a_xip, 1)
                    for bb in range(2):
                        for c in range(2, 4):
                            last = nc.tensor.matmul(PS[:, 4 * bb + c, :], win_s[:, c * P:(c + 1) * P], xnT[:, bb],
                                                    start=True, stop=True)
                        last.then_inc(a_zp, 1)
                    for bb in range(2):
                        pe.wait_ge(a_u, 2 * it + bb + 1)
                        for h in range(HALVES):
                            last = nc.tensor.matmul(PS[0:R, 4 * bb, :], wx_s[:, h, 0:R], u_s[:, bb, h],
                                                    start=(h == 0), stop=(h == 1))
                        last.then_inc(a_dtp, 1)
                        for h in range(HALVES):
                            last = nc.tensor.matmul(PS[:, 4 * bb + 1, :], wx_s[:, h, R:], u_s[:, bb, h],
                                                    start=(h == 0), stop=(h == 1))
                        last.then_inc(a_xp, 1)
                    for bb in range(2):
                        pe.wait_ge(a_dtr, 2 * it + bb + 1)
                        pe.wait_ge(a_sz, 2 * it + bb + 1)
                        for h in range(HALVES):
                            last = nc.tensor.matmul(PS[:, 4 * bb + 2 + h, :], wdt_s[0:R, h * P:(h + 1) * P],
                                                    dtr_s[0:R, bb, :], start=True, stop=True)
                        last.then_inc(a_v, 1)
            pe.wait_ge(a_v, 8)
            pe.sem_inc(a_end, 1)

            def sum_states(m, kk, part):
                if part == 0:
                    blk = m * NBLK + kk
                    pe.wait_ge(scan_done, (blk + 1) * NQ)
                    pe.wait_ge(evacuated, blk - 1 + EV0)
                    if kk == 0:
                        pe.wait_ge(c_spread, 2 * m + 2)
                for step in range(part * TC // SUM_PARTS, (part + 1) * TC // SUM_PARTS):
                    s, i, j = step // 64, step % 64 // 4, step % 4
                    t = s * 64 + j * 16 + i
                    last = nc.tensor.matmul(PS[32 * j:32 * j + 32, 4 + kk, s * DB:(s + 1) * DB],
                                            cd[:, s * 4 + j, 32 * i:32 * i + 32], seg(hb[:, kk])[:, :, 1 + t],
                                            start=(i == 0), stop=(i == 15), tile_position=(0, 32 * j))
                if part == SUM_PARTS - 1:
                    last.then_inc(y_done, 1)

            def turn(m, part):
                if part == 0:
                    pe.wait_ge(evacuated, (m + 1) * NBLK + EV0)
                h, s = part // TS, part % TS
                last = nc.tensor.transpose(PS[:, 6, part * P:(part + 1) * P], ysb[:, s, h * P:(h + 1) * P],
                                           ident_s[:])
                if part == HALVES * TS - 1:
                    last.then_inc(post_t, 1)

            def project(m, s):
                pe.wait_ge(g_done, m + 1)
                for h in range(HALVES):
                    last = nc.tensor.matmul(PS[:, 7, s * P:(s + 1) * P], G[:, h, s * P:(s + 1) * P],
                                            wout_s[:, h], start=(h == 0), stop=(h == 1))
                if s == TS - 1:
                    last.then_inc(out_ready, 1)

            def spread_delta(blk, kk, p, reused):
                if reused:
                    pe.wait_ge(exp_done, blk * NP + p - 1)
                i, g = p % RI, p // RI
                nc.tensor.matmul(PS[:, p % 2, :], selb[:, i * P:(i + 1) * P], rows[0:ROWS, kk, g, :],
                                 start=True, stop=True).then_inc(arg_ready, 1)

            def spread_du(blk, kk, p, reused):
                if reused:
                    pe.wait_ge(mult_done, blk * NP + p - 1)
                i, g = p % RI, p // RI
                nc.tensor.matmul(PS[:, 2 + p % 2, :], selb[:, i * P:(i + 1) * P], rows[0:ROWS, kk, NRT + g, :],
                                 start=True, stop=True).then_inc(du_ready, 1)

            def emit(m, kk, before, post):
                blk = m * NBLK + kk
                pe.wait_ge(rows_in[kk], 64 * m + 64)
                for p in range(NP):
                    spread_delta(blk, kk, p, before or p > 1)
                    if p >= LEAD:
                        spread_du(blk, kk, p - LEAD, before or p - LEAD > 1)
                    elif before:
                        spread_du(blk - 1, 1 - kk, NP + p - LEAD, 1)
                    if post and 0 <= p - P_TURN < HALVES * TS:
                        turn(m - 1, p - P_TURN)
                    if post and 0 <= p - P_PROJECT < TS:
                        project(m - 1, p - P_PROJECT)
                    if before and 0 <= p - P_SUM < SUM_PARTS:
                        sum_states(m if kk else m - 1, 1 - kk, p - P_SUM)

            def tail(m):
                for p in range(NP - LEAD, NP):
                    spread_du(m * NBLK + NBLK - 1, NBLK - 1, p, 1)
                for part in range(SUM_PARTS):
                    sum_states(m, NBLK - 1, part)
                for part in range(HALVES * TS):
                    turn(m, part)
                for s in range(TS):
                    project(m, s)

            run_blocks(pe, emit, tail)

            def stage_xh(n):
                pe.wait_ge(f_xn, n + 1)
                for s in range(GT):
                    last = nc.tensor.transpose(PS[:, 5, s * P:(s + 1) * P], xhs[:, s], ident_s[:])
                last.then_inc(f_xhT, 1)

            def bias_of_offset(l, pair, lp):
                pe.wait_ge(f_w[lp], F_LOADS * (pair + 1))
                for ec in range(E * GT):
                    e, c = ec // GT, ec % GT
                    last = nc.tensor.matmul(PS[:, 4, ec:ec + 1], w1_s[:, lp, e, c * P:(c + 1) * P],
                                            lb_s[:, bass.ds(l * E + e, 1)], start=True, stop=True)
                last.then_inc(f_bp, 1)
                pe.wait_ge(f_bias, l + 1)

            def first(n, lp, gp, e):
                for c in range(GT):
                    i = E * GT * n + GT * e + c
                    pe.wait_ge(f_gelu, i + (3 if e == c == 0 else 1))
                    for part_w, part_x in ((0, 0), (0, 1), (1, 0)):
                        last = nc.tensor.matmul(PS[:, HIDDEN[(GT * e + c) % 3], :],
                                                w1p[:, lp, part_w, e, c * P:(c + 1) * P],
                                                xhT[:, gp, part_x],
                                                start=(part_w + part_x == 0), stop=(part_w == 1))
                    last.then_inc(f_h, 1)

            def second(n, lp, e):
                pe.wait_ge(f_gelu, E * GT * n + GT * e + GT + 3)
                pe.wait_ge(f_sum, FS0 + E * n + e - 1)
                for s in range(GT):
                    for c in range(GT):
                        last = nc.tensor.matmul(PS[:, 2 + e % 2, s * P:(s + 1) * P], hT[:, e % 2, c, s * P:(s + 1) * P],
                                                w2_s[:, lp, e * GT + c], start=(c == 0), stop=(c == GT - 1))
                last.then_inc(f_y, 1)

            def begin(first_layer):
                bias_of_offset(*first_layer)
                stage_xh(0)
                pe.wait_ge(f_xhTs, 1)

            def step(layer, g, gp, new, more):
                l, pair, lp = layer
                n = l * NG + g
                if isinstance(g, int) and g == 0:
                    pe.wait_ge(f_wp, l * E + E)
                pe.wait_ge(f_xhTs, n + 1)
                first(n, lp, gp, 0)
                if new:
                    bias_of_offset(*new)
                first(n, lp, gp, 1)
                second(n, lp, 0)
                if more:
                    stage_xh(n + 1)
                first(n, lp, gp, 2)
                second(n, lp, 1)
                first(n, lp, gp, 3)
                second(n, lp, 2)
                second(n, lp, 3)

            run_layers(pe, begin, step)

        @block.vector
        def _(dve):
            def moments(link, links, src, st, mv, rs, tiles, asked):
                for s in range(tiles):
                    last = nc.vector.bn_stats(st[:, s, :], src(s))
                last.then_inc(link, 1)
                dve.wait_ge(link, links + 1)
                apart(dve)
                for s in range(tiles):
                    last = nc.vector.bn_aggr(mv[:, s, :], st[:, s, :])
                last.then_inc(link, 1)
                dve.wait_ge(link, links + 2)
                nc.vector.tensor_scalar(rs, mv[:, :, 1], EPS, None, ALU.add).then_inc(asked, 1)

            def scaled(src, mv, rs, dst, tiles):
                for s in range(tiles):
                    last = nc.vector.tensor_scalar(dst(s), src(s), mv[:, s, 0:1], rs[:, s:s + 1],
                                                   ALU.subtract, ALU.mult)
                return last

            def normalise(link, links, src, st, mv, rs, dst, tiles, asked, answered, count):
                moments(link, links, src, st, mv, rs, tiles, asked)
                dve.wait_ge(answered, count)
                return scaled(src, mv, rs, dst, tiles)

            def normalise_x(it):
                for bb in range(2):
                    dve.wait_ge(a_x[bb], 16 * it + 16)
                    moments(a_link, (2 * it + bb) * 2, lambda s: xt[:, bb, s], st_a[:, bb], mv_a[:, bb],
                            rs_a[:, bb], 4, a_var)
                dve.wait_ge(a_tp, 2 * it + 2)
                for bb in range(2):
                    dve.wait_ge(a_rs, 2 * it + bb + 1)
                    scaled(lambda s: xt[:, bb, s], mv_a[:, bb], rs_a[:, bb], lambda s: xn[:, bb, s], 4
                           ).then_inc(a_xn, 1)

            normalise_x(0)
            dve.wait_ge(weights, 16 * 13)
            dve.wait_ge(a_start, 1)
            nc.vector.tensor_scalar(A_s[:], A_s[:], -1.0, None, ALU.mult).then_inc(prepared, 1)
            nc.vector.tensor_copy(selb[:], sel_t[0:ROWS, :]).then_inc(prepared, 1)
            dve.wait_ge(a_pad, 1)
            with dve.Fori(0, BP) as bp:
                for half in range(2):
                    it = bp * 2 + half
                    for bb in range(2):
                        dve.wait_ge(a_xi, 2 * it + bb + 1)
                        for t in range(KC):
                            for h in range(HALVES):
                                tap = chan_s[:, h, t:t + 1]
                                if t == 0:
                                    last = nc.vector.tensor_scalar(conv[:, bb, h], xi[:, bb, h, t:t + TT], tap, None,
                                                                   ALU.mult)
                                else:
                                    last = nc.vector.scalar_tensor_tensor(conv[:, bb, h], xi[:, bb, h, t:t + TT], tap,
                                                                          conv[:, bb, h], ALU.mult, ALU.add)
                            if t < KC - 1:
                                last.then_inc(a_tap, 1)
                                dve.wait_ge(a_tap, (2 * it + bb) * (KC - 1) + t + 1)
                            else:
                                last.then_inc(a_conv, 1)
                        dve.wait_ge(a_conv, 2 * (2 * it + bb) + 1)
                        pad = xi[:, bb, :, 0:KC - 1]
                        if half == 0:
                            nc.vector.tensor_copy(pad, xi[:, bb, :, TT:]).then_inc(a_conv, 1)
                        else:
                            nc.vector.memset(pad, 0.0).then_inc(a_conv, 1)
                    for bb in range(2):
                        dve.wait_ge(a_xp, 2 * it + bb + 1)
                        nc.vector.tensor_copy(bc_t[:, bb], PS[:, 4 * bb + 1, :]).then_inc(a_bc, 1)
                    normalise_x(it + 1)
                    for bb in range(2):
                        dve.wait_ge(a_mag, 4 * it + 1 + bb)
                        for h in range(HALVES):
                            last = nc.vector.tensor_scalar(rl[:, bb, h], PS[:, 4 * bb + 2 + h, :],
                                                           chan_s[:, h, KC + 1:KC + 2], 0.0, ALU.add, ALU.max)
                        last.then_inc(a_rl, 1)
                    for bb in range(2):
                        dve.wait_ge(a_mag, 4 * it + 3 + bb)
                        nc.vector.tensor_scalar(one_p[:, bb], mag[:, bb], 1.0, None, ALU.add).then_inc(a_onep, 1)
                    for bb in range(2):
                        dve.wait_ge(a_onep, 2 * it + bb + 1)
                        nc.vector.scalar_tensor_tensor(slip[:, bb], one_p[:, bb], 1.0, mag[:, bb], ALU.subtract,
                                                       ALU.subtract).then_inc(a_slip, 1)
                    for bb in range(2):
                        dve.wait_ge(a_ln, 2 * it + bb + 1)
                        dve.wait_ge(a_slip, 2 * it + bb + 1)
                        nc.vector.tensor_tensor(lg[:, bb], lg[:, bb], slip[:, bb], ALU.subtract).then_inc(a_exact, 1)
                    for bb in range(2):
                        dve.wait_ge(a_exact, 2 * it + bb + 1)
                        dve.wait_ge(a_rl, 2 * it + bb + 3)
                        nc.vector.tensor_tensor(dd[:, bb, 0], lg[:, bb], rl[:, bb], ALU.add).then_inc(a_delta, 1)
                    for bb in range(2):
                        dve.wait_ge(a_delta, 2 * it + bb + 1)
                        nc.vector.tensor_tensor(dd[:, bb, 1], dd[:, bb, 0], u_s[:, bb], ALU.mult).then_inc(a_du, 1)
                    for bb in range(2):
                        dve.wait_ge(a_p1, 2 * it + bb + 1)
                        nc.vector.tensor_tensor(rest[:, bb], dd[:, bb], part[bb][0], ALU.subtract).then_inc(a_rest, 1)
            dve.wait_ge(a_du, 2 * NIT)
            dve.sem_inc(a_end, 1)
            dve.wait_ge(a_xn, 2 * NIT + 2)
            dve.wait_ge(a_p3, 2 * NIT + 2)
            dve.wait_ge(a_end, 4)

            def skip(m):
                dve.wait_ge(post_in, 96 * m + 96)
                dve.wait_ge(post_t, m + 2)
                for h in range(HALVES):
                    last = nc.vector.scalar_tensor_tensor(by_step(G[:, h]), by_token(usz[:, 0, h]),
                                                          chan_s[:, h, KC + 2:KC + 3],
                                                          by_step(PS[:, 6, h * TS * P:(h + 1) * TS * P]),
                                                          ALU.mult, ALU.add)
                last.then_inc(skipped, 1)

            def chunk_stats(m):
                dve.wait_ge(out_ready, m + 1)
                nc.vector.scalar_tensor_tensor(xsum, xres, 2.0,
                                               PS[:, 7, 0:TS * H].rearrange("p (s h) -> p s h", h=H),
                                               ALU.mult, ALU.add).then_inc(p_link, 1)
                dve.wait_ge(p_link, m * P_LINKS + 1)
                moments(p_link, m * P_LINKS + 1, lambda s: xsum[:, s], st_m, mv_m, rs_m, TS, p_var)

            def chunk_norm(m):
                dve.wait_ge(x1_out, 16 * m + X0)
                dve.wait_ge(p_rs, m + 1)
                scaled(lambda s: xsum[:, s], mv_m, rs_m, lambda s: x1c[:, s], TS).then_inc(post_done, 1)

            def emit(m, kk, before, post):
                blk = m * NBLK + kk
                dve.wait_ge(bc_in, 32 * (m + 1))
                Bc = bc[:, bass.ds(m % 2 * 2 * TC, TC)].unsqueeze(1).broadcast_to([P, CB, TC])

                def times_b(q, r):
                    if before or q > 1:
                        dve.wait_ge(scan_done, blk * NQ + q - 1)
                    dve.wait_ge(du_ready, blk * NP + 2 * q + r + 1 + DU0)
                    nc.vector.tensor_tensor(seg(dB[:, q % 2])[:, r * CB:(r + 1) * CB, 1:],
                                            PS[:, 2 + r, :].rearrange("p (c t) -> p c t", c=CB), Bc,
                                            ALU.mult).then_inc(mult_done, 1)

                times_b(0, 0)
                for q in range(NQ):
                    times_b(q, 1)
                    if q < NQ - 1:
                        times_b(q + 1, 0)
                    dve.wait_ge(mult_done, blk * NP + 2 * q + 2)
                    dve.wait_ge(exp_done, blk * NP + 2 * q + 2)
                    dve.wait_ge(slot_ready, blk * NQ + q + 1)
                    if q == 0 and kk == 1 and isinstance(m, int):
                        dve.wait_ge(a_rows, NIT * 16 * ROW_STORES + 16)
                    if q == 0:
                        dve.wait_ge(y_done, blk - 1 + Y0)
                        dve.wait_ge(carried, blk - 1 + CARRY0)
                    nc.vector.tensor_tensor_scan(hb[:, kk, q * QD * SEG:(q + 1) * QD * SEG], dA[:, q % 2],
                                                 dB[:, q % 2], 0.0, ALU.mult, ALU.add).then_inc(scan_done, 1)
                    if post and q == Q_GATE:
                        skip(m - 1)
                    if post and q == Q_STATS:
                        chunk_stats(m - 1)
                    if post and q == Q_STATS + 1:
                        chunk_norm(m - 1)

            def split_w1(l, lp):
                for e in range(E):
                    dve.wait_ge(f_g, E * l + e + 1)
                    nc.vector.tensor_copy(w1p[:, lp, 0, e], w1g[:, e]).then_inc(f_upper, 1)
                for e in range(E):
                    dve.wait_ge(f_upper, E * l + e + 1)
                    nc.vector.tensor_tensor(w1p[:, lp, 1, e], w1g[:, e], w1p[:, lp, 0, e].bitcast(fp32), ALU.subtract
                                            ).then_inc(f_wp, 1)

            def tail(m):
                dve.wait_ge(scan_done, NCH * NBLK * NQ)
                split_w1(0, 0)
                skip(m)
                chunk_stats(m)
                chunk_norm(m)

            run_blocks(dve, emit, tail)
            dve.wait_ge(carried, NCH * NBLK + CARRY0)

            dve.wait_ge(post_done, NCH + POST0)
            dve.wait_ge(f_w[0], F_LOADS)
            nc.vector.memset(order, 0.0).then_inc(f_sum, FS0)
            dve.wait_ge(f_sum, FS0)
            dve.wait_ge(x_in, 16)
            nc.vector.tensor_copy(X[:, NT - TS:], x1c).then_inc(f_last, 1)
            dve.wait_ge(f_last, 1)

            F_LINKS = 12

            def at(v, g, s):
                return v[:, bass.ds(g * GT + s, 1), :].rearrange("p a h -> p (a h)")

            def stage_norm(n, g):
                dve.wait_ge(f_sum, E * n + E)
                dve.wait_ge(f_xhT, n + XH0)
                normalise(f_link, n * F_LINKS, lambda s: at(X, g, s), st_f, mv_f, rs_f, lambda s: xhs[:, s], GT,
                          f_var, f_rs, n + 1).then_inc(f_xn, 1)

            def each(v):
                return v.unsqueeze(2).broadcast_to([P, GT, E])

            def stage_scores(n, l):
                dve.wait_ge(f_scored, n + 1)
                dve.wait_ge(f_rt, n + LG0)
                nc.vector.reduce_sum(lgt, scored, AX.X).then_inc(f_lm, 1)
                dve.wait_ge(f_lm, n + 1 + LG0)
                nc.vector.tensor_tensor(lgt, lgt, rb_s[:, bass.ds(l * E, E)].unsqueeze(1).broadcast_to([P, GT, E]),
                                        ALU.add).then_inc(f_link, 1)
                dve.wait_ge(f_link, n * F_LINKS + 3)
                nc.vector.reduce_max(mx, lgt, AX.X).then_inc(f_link, 1)
                dve.wait_ge(f_link, n * F_LINKS + 4)
                nc.vector.tensor_tensor(lgt, lgt, each(mx), ALU.subtract).then_inc(f_lg, 1)

            def stage_router(n, gp):
                dve.wait_ge(f_rt, n + 1 + LG0)
                nc.vector.reduce_sum(sm, ex, AX.X).then_inc(f_link, 1)
                dve.wait_ge(f_link, n * F_LINKS + 5)
                nc.vector.reciprocal(sm, sm).then_inc(f_link, 1)
                dve.wait_ge(f_link, n * F_LINKS + 6)
                nc.vector.tensor_tensor(pr, ex, each(sm), ALU.mult).then_inc(f_link, 1)
                dve.wait_ge(f_link, n * F_LINKS + 7)
                for j in range(E):
                    pj = pr[:, :, j:j + 1]
                    if j > 0:
                        last = nc.vector.tensor_tensor(order[:, :, j, 0:j], pj.broadcast_to([P, GT, j]),
                                                       pr[:, :, 0:j], ALU.is_gt)
                    if j < E - 1:
                        last = nc.vector.tensor_tensor(order[:, :, j, j + 1:], pj.broadcast_to([P, GT, E - 1 - j]),
                                                       pr[:, :, j + 1:], ALU.is_ge)
                last.then_inc(f_link, 1)
                dve.wait_ge(f_link, n * F_LINKS + 8)
                nc.vector.reduce_sum(rank, order.rearrange("p s j e -> p s e j"), AX.X).then_inc(f_link, 1)
                dve.wait_ge(f_link, n * F_LINKS + 9)
                nc.vector.scalar_tensor_tensor(selp, rank, 2.0, pr, ALU.is_lt, ALU.mult).then_inc(f_link, 1)
                dve.wait_ge(f_link, n * F_LINKS + 10)
                nc.vector.reduce_sum(sm, selp, AX.X).then_inc(f_link, 1)
                dve.wait_ge(f_link, n * F_LINKS + 11)
                nc.vector.reciprocal(sm, sm).then_inc(f_link, 1)
                dve.wait_ge(f_link, n * F_LINKS + 12)
                cw = comb[:, gp].rearrange("p (s e) -> p s e", e=E)
                nc.vector.tensor_tensor(cw, selp, each(sm), ALU.mult).then_inc(f_cw, 1)
                dve.wait_ge(f_cw, n + 1)
                nc.vector.reduce_sum(csum[:, gp], cw, AX.X).then_inc(f_cs, 1)

            def sum_bias(n):
                dve.wait_ge(f_weighted, n + 1)
                dve.wait_ge(f_x0, n + 1)
                nc.vector.reduce_sum(bias2, weighted.rearrange("p s e h -> p s h e"), AX.X).then_inc(f_yb, 1)

            def start_sum(n, g, gp):
                dve.wait_ge(f_yb, n + 2)
                dve.wait_ge(f_cs, n + 1)
                for s in range(GT):
                    last = nc.vector.scalar_tensor_tensor(at(X, g, s), at(X, g, s), csum[:, gp, s:s + 1],
                                                          bias2[:, s], ALU.mult, ALU.add)
                last.then_inc(f_x0, 1)

            def add_expert(n, g, gp, e):
                dve.wait_ge(f_y, FY0 + E * n + e + 1)
                dve.wait_ge(f_x0, n + 2)
                dve.wait_ge(f_sum, FS0 + E * n + e)
                for s in range(GT):
                    last = nc.vector.scalar_tensor_tensor(at(X, g, s), PS[:, 2 + e % 2, s * P:(s + 1) * P],
                                                          comb[:, gp, s * E + e:s * E + e + 1], at(X, g, s),
                                                          ALU.mult, ALU.add)
                last.then_inc(f_sum, 1)

            def split_xh(n, gp):
                dve.wait_ge(f_xhT, n + 1 + XH0)
                nc.vector.tensor_copy(xhT[:, gp, 0], PS[:, 5, :]).then_inc(f_xhu, 1)
                dve.wait_ge(f_xhu, n + 1)
                nc.vector.tensor_tensor(xhT[:, gp, 1], PS[:, 5, :], xhT[:, gp, 0].bitcast(fp32), ALU.subtract).then_inc(f_xhTs, 1)

            def add_bias(l, lp):
                dve.wait_ge(f_bp, l + 1)
                nc.vector.tensor_tensor(bias1[:, lp], PS[:, 4, 0:E * GT], b1_s[:, bass.ds(l * E * GT, E * GT)],
                                        ALU.add).then_inc(f_bias, 1)

            O_LINKS = 3

            def finish(g, gp):
                dve.wait_ge(x_in, 32)
                dve.wait_ge(f_sum, FS0 + E * (NG * (NL - 1) + g + 1))
                dve.wait_ge(f_fin, g + FIN0)
                tiles = lambda v: v[:, bass.ds(g * GT, GT), :]
                nc.vector.tensor_tensor(xsum_o, tiles(X), tiles(X1), ALU.add).then_inc(f_fl, 1)
                dve.wait_ge(f_fl, g * O_LINKS + 1)
                dve.wait_ge(f_out[gp], 64 * (g // 2) + 64)
                normalise(f_fl, g * O_LINKS + 1, lambda s: xsum_o[:, s], st_o, mv_o, rs_o, lambda s: xo[:, gp, s],
                          GT, o_var, o_rs, g + 1).then_inc(f_fin, 1)

            def last_layer(l):
                return isinstance(l, int) and l == NL - 1

            def begin(first_layer):
                add_bias(0, 0)
                stage_norm(0, 0)
                split_xh(0, 0)
                stage_scores(0, 0)
                stage_router(0, 0)
                sum_bias(0)

            def step(layer, g, gp, new, more):
                l, pair, lp = layer
                n = l * NG + g
                next_l, _, next_lp = new or layer
                if new:
                    add_bias(next_l, next_lp)
                if more:
                    stage_norm(n + 1, 0 if new else g + 1)
                start_sum(n, g, gp)
                add_expert(n, g, gp, 0)
                if more:
                    split_xh(n + 1, 1 - gp)
                    stage_scores(n + 1, next_l)
                add_expert(n, g, gp, 1)
                if more:
                    stage_router(n + 1, 1 - gp)
                add_expert(n, g, gp, 2)
                if new:
                    split_w1(next_l, next_lp)
                if more:
                    sum_bias(n + 1)
                if last_layer(l) and not (isinstance(g, int) and g == 0):
                    finish(g - 1, 1 - gp)
                add_expert(n, g, gp, 3)

            run_layers(dve, begin, step)

            finish(NG - 1, 1)


_INS = ["x", "vecs", "chan", "a_log", "ident", "sel", "w_in", "w_xproj", "w_dt", "w_out",
        "router_w", "router_b", "ln_g", "ln_b", "w1", "b1", "w2", "b2"]


def kernel(L0_attn_x, L0_attn_ln_w, L0_attn_ln_b, L0_attn_W_in, L0_attn_conv_w, L0_attn_conv_b, L0_attn_W_xproj,
           L0_attn_W_dt, L0_attn_b_dt, L0_attn_A_log, L0_attn_D, L0_attn_W_out, L0_ffn_router_w, L0_ffn_router_b,
           L0_ffn_ln_g, L0_ffn_ln_b, L0_ffn_w1, L0_ffn_b1, L0_ffn_w2, L0_ffn_b2):
    import concourse.bacc as bacc
    from concourse.bass_utils import run_bass_kernel_spmd

    f = lambda v: np.asarray(v)
    halves = lambda v: f(v).reshape(HALVES, P).T[:, :, None]
    sel = np.zeros((PARTS, 2, RI, RI, 2, N), np.float32)
    for b in range(2):
        for i in range(RI):
            sel[:, b, i, i, b, :] = 1.0
    data = {
        "x": f(L0_attn_x),
        "vecs": np.stack([f(L0_attn_ln_w), f(L0_attn_ln_b)], 1),
        "chan": np.concatenate([f(L0_attn_conv_w).reshape(HALVES, P, KC).transpose(1, 0, 2), halves(L0_attn_conv_b),
                                halves(L0_attn_b_dt), halves(L0_attn_D)], 2),
        "a_log": np.concatenate([f(L0_attn_A_log).T] * 2, 0),
        "ident": np.eye(P, dtype=np.float32),
        "sel": sel.reshape(ROWS, RI * P),
        "w_in": f(L0_attn_W_in), "w_xproj": f(L0_attn_W_xproj), "w_dt": f(L0_attn_W_dt), "w_out": f(L0_attn_W_out),
        "router_w": np.concatenate([f(L0_ffn_router_w).transpose(0, 2, 1).reshape(1, NL * E * H)] * P, 0),
        "router_b": np.concatenate([f(L0_ffn_router_b).reshape(1, NL * E)] * P, 0),
        "ln_g": f(L0_ffn_ln_g).reshape(NL * E, H).T,
        "ln_b": f(L0_ffn_ln_b).reshape(NL * E, H).T,
        "w1": f(L0_ffn_w1),
        "b1": f(L0_ffn_b1).reshape(NL * E * GT, P).T,
        "w2": f(L0_ffn_w2),
        "b2": np.concatenate([f(L0_ffn_b2).reshape(1, NL * E * H)] * P, 0),
    }
    nc = bacc.Bacc("TRN2", target_bir_lowering=False, num_devices=1)
    arrays, args = {}, []
    for name in _INS:
        a = np.ascontiguousarray(data[name])
        arrays[f"in_{name}"] = a
        args.append(nc.dram_tensor(f"in_{name}", a.shape, mybir.dt.from_np(a.dtype), kind="ExternalInput").ap())
    out = nc.dram_tensor("out_dram", (B, L, H), mybir.dt.float32, kind="ExternalOutput").ap()
    build(nc, *args, out)
    r = run_bass_kernel_spmd(nc, [arrays], core_ids=[0])
    return r.results[0]["out_dram"]
```
